# Optimizing a Trainium2 kernel written in Bass

```python
import numpy as np
import jax
import jax.numpy as jnp

def _softmax(x, axis=-1):
    return jax.nn.softmax(x, axis=axis)

def _gelu(x):
    return jax.nn.gelu(x, approximate=True)

def _silu(x):
    return jax.nn.silu(x)

def _sigmoid(x):
    return jax.nn.sigmoid(x)

def _layernorm(x, axis=-1, eps=1e-05):
    m = jnp.mean(x, axis=axis, keepdims=True)
    v = jnp.var(x, axis=axis, keepdims=True)
    return (x - m) / jnp.sqrt(v + eps)

def _scatter_add(tgt, idx, src, axis=0):
    return tgt.at[idx].add(src)

def _segment_sum(src, seg, n):
    return jax.ops.segment_sum(src, seg, n)
kernel_name = 'mk_gnn_preln_d2_gnn_r8_2d8234'

def setup_inputs(seed: int=0):
    np.random.seed(seed)
    _w = jnp.asarray

    def _rec_inputs():
        import jax
        import jax.numpy as jnp
        _gk = jax.random.key(seed)
        x = -8.776e-05 + 1 * jax.random.normal(jax.random.fold_in(_gk, 1), (6250, 512), jnp.float32)
        src = jax.random.randint(jax.random.fold_in(_gk, 2), (100000,), 0, 6250, jnp.int32)
        dst = jnp.minimum((6250 * jax.random.uniform(jax.random.fold_in(_gk, 3), (100000,)) ** 2.0).astype(jnp.int32), 49999)
        _o = jnp.argsort(dst, stable=True)
        src = src[_o]
        dst = dst[_o]
        return (x, src, dst)
    x, src, dst = _rec_inputs()

    def _L0_gnn_setup():
        import jax, jax.numpy as jnp
        import numpy as np
        N_NODES = 1250
        N_EDGES = 20000
        D_IN = 512
        D_OUT = 512
        key = jax.random.key(seed)
        k1, k2, k3 = jax.random.split(key, 3)
        x = jax.random.normal(k1, (N_NODES, D_IN), dtype=jnp.float32)
        W = jax.random.normal(k2, (D_IN, D_OUT), dtype=jnp.float32) * (1.0 / np.sqrt(D_IN))
        b = jnp.zeros((D_OUT,), dtype=jnp.float32)
        edge_index = jax.random.randint(k3, (2, N_EDGES), 0, N_NODES, dtype=jnp.int32)
        return {'x': x, 'W': W, 'b': b, 'edge_index': edge_index}
    _L0_gnn_all = _L0_gnn_setup()
    _L0_gnn_in = {k: v for k, v in _L0_gnn_all.items() if k in ('W', 'b')}
    del _L0_gnn_all

    def _L1_gnn_setup():
        import jax, jax.numpy as jnp
        import numpy as np
        LN_EPS = 1e-05
        key = jax.random.key(seed)
        k1, k2, k3, k4 = jax.random.split(key, 4)
        N, D, E = (1250, 512, 18750)
        scale = 1.0 / np.sqrt(D)
        return {'node_feature': jax.random.normal(k1, (N, D), dtype=jnp.float32), 'edge_index': jax.random.randint(k2, (2, E), 0, N, dtype=jnp.int64), 'ln_gamma': jnp.ones((D,), dtype=jnp.float32), 'ln_beta': jnp.zeros((D,), dtype=jnp.float32), 'w_l': jax.random.normal(k3, (D, D), dtype=jnp.float32) * scale, 'b_l': jnp.zeros((D,), dtype=jnp.float32), 'w_r': jax.random.normal(k4, (D, D), dtype=jnp.float32) * scale}
    _L1_gnn_all = _L1_gnn_setup()
    _L1_gnn_in = {k: v for k, v in _L1_gnn_all.items() if k in ('ln_gamma', 'ln_beta', 'w_l', 'b_l', 'w_r')}
    del _L1_gnn_all
    return {'x': x, 'src': src, 'dst': dst, 'L0_gnn_W': _L0_gnn_in['W'], 'L0_gnn_b': _L0_gnn_in['b'], 'L1_gnn_ln_gamma': _L1_gnn_in['ln_gamma'], 'L1_gnn_ln_beta': _L1_gnn_in['ln_beta'], 'L1_gnn_w_l': _L1_gnn_in['w_l'], 'L1_gnn_b_l': _L1_gnn_in['b_l'], 'L1_gnn_w_r': _L1_gnn_in['w_r']}

def reference(x, src, dst, L0_gnn_W, L0_gnn_b, L1_gnn_ln_gamma, L1_gnn_ln_beta, L1_gnn_w_l, L1_gnn_b_l, L1_gnn_w_r):
    import jax
    import jax.numpy as jnp

    def _L0_gnn_ref(x, W, b, edge_index):
        import jax, jax.numpy as jnp
        import numpy as np
        N_NODES = 1250
        N_EDGES = 20000
        D_IN = 512
        D_OUT = 512
        N = x.shape[0]
        self_loops = jnp.arange(N, dtype=edge_index.dtype)
        src = jnp.concatenate([edge_index[0], self_loops])
        dst = jnp.concatenate([edge_index[1], self_loops])
        ones = jnp.ones(src.shape[0], dtype=x.dtype)
        deg = jax.ops.segment_sum(ones, dst, num_segments=N)
        dinv_sqrt = jnp.where(deg > 0, jax.lax.rsqrt(deg), 0.0)
        norm = dinv_sqrt[src] * dinv_sqrt[dst]
        h = x @ W
        msgs = h[src] * norm[:, None]
        agg = jax.ops.segment_sum(msgs, dst, num_segments=N)
        return jax.nn.relu(agg + b)

    def _L1_gnn_ref(node_feature, edge_index, ln_gamma, ln_beta, w_l, b_l, w_r):
        import jax, jax.numpy as jnp
        import numpy as np
        LN_EPS = 1e-05
        N = node_feature.shape[0]
        residual = node_feature
        mu = jnp.mean(node_feature, axis=-1, keepdims=True)
        var = jnp.mean(jnp.square(node_feature - mu), axis=-1, keepdims=True)
        x = (node_feature - mu) * jax.lax.rsqrt(var + LN_EPS) * ln_gamma + ln_beta
        src, dst = (edge_index[0], edge_index[1])
        msg = x[src]
        summed = jax.ops.segment_sum(msg, dst, num_segments=N)
        cnt = jax.ops.segment_sum(jnp.ones_like(dst, dtype=x.dtype), dst, num_segments=N)
        agg = summed / jnp.maximum(cnt, 1.0)[:, None]
        out = agg @ w_l.T + b_l + x @ w_r.T
        out = jax.nn.relu(out)
        return out + residual
    edge_index = jnp.stack([src, dst])
    h = jnp.maximum(_layernorm(x, axis=-1), 0.0)
    x = x + _L0_gnn_ref(h, L0_gnn_W, L0_gnn_b, edge_index)
    h = jnp.maximum(_layernorm(x, axis=-1), 0.0)
    x = x + _L1_gnn_ref(h, edge_index, L1_gnn_ln_gamma, L1_gnn_ln_beta, L1_gnn_w_l, L1_gnn_b_l, L1_gnn_w_r)
    return x

_drawn_inputs = setup_inputs


def setup_inputs(seed=0):
    import zlib

    import numpy as np

    out = dict(_drawn_inputs(seed))
    spreads = {'L0_gnn_b': (0.0, 0.1),
     'L1_gnn_ln_gamma': (1.0, 0.2),
     'L1_gnn_ln_beta': (0.0, 0.1),
     'L1_gnn_b_l': (0.0, 0.1)}
    factors = {}
    for name, (base, spread) in spreads.items():
        noise = np.random.default_rng([zlib.crc32(name.encode()), seed]).standard_normal(out[name].shape)
        drawn = base * np.exp(spread * noise) if base else spread * noise
        out[name] = jnp.asarray(drawn.astype(out[name].dtype))
    for name, factor in factors.items():
        out[name] = (out[name] * factor).astype(out[name].dtype)
    return out
```

```python
from contextlib import ExitStack

import concourse.bass as bass
from concourse import mybir

ALU = mybir.AluOpType
ACT = mybir.ActivationFunctionType
F32 = mybir.dt.float32
F16 = mybir.dt.float16
I32 = mybir.dt.int32
U32 = mybir.dt.uint32

P = 128
RING = 16
WAIT_EVERY = 4
SRING = 32
EPS = 1e-5
UP = 2048.0
HIST_COLS = 40
X_GROUP = 7


def ds(start, size):
    return bass.ds(start, size)


def gnn_kernel(nc, x, src, dst, W0, b0, gamma, beta, w_l, b_l, w_r, out):
    N, D = x.shape
    E = src.shape[0]
    KC = D // P
    NT = (N + P - 1) // P
    LAST = N - (NT - 1) * P
    NB = (E + P - 1) // P
    FULLB = E // P
    BC = (NB + P - 1) // P
    STEPS = NB + NT - 1
    GROUPS = (NB + RING - 1) // RING
    HP = 125
    HC = E // HP
    CHUNKS = HC // HIST_COLS
    XG = NT // X_GROUP
    DIG = NT + P
    assert HP * HC == E and CHUNKS * HIST_COLS == HC and XG * X_GROUP == NT and D == 512

    table = [nc.dram_tensor(f"table{n}", [NT * P, 2 * D], F16, kind="Internal").ap() for n in range(2)]
    xT_dram = nc.dram_tensor("xT_dram", [NT * P, D], F32, kind="Internal").ap()

    with ExitStack() as ctx:
        def sb(name, shape, dt):
            return ctx.enter_context(nc.sbuf_tensor(name, shape, dt))

        def bank(name):
            return ctx.enter_context(nc.psum_tensor(name, [P, 512], F32))

        def sem(name):
            return ctx.enter_context(nc.semaphore(name))

        nodes = sb("nodes", [P, NT * D], F32)
        nodes16 = nodes[:, :].bitcast(F16)
        ring = sb("ring", [P, RING * 2 * D], F16)
        sel = sb("sel", [P, SRING * P], F16)
        weights = sb("weights", [P, 3 * KC * D], F32)
        w0_sb, wl_sb, wr_sb = (weights[:, n * KC * D:(n + 1) * KC * D] for n in range(3))
        b0_sb = sb("b0_sb", [P, D], F32)
        Bl = sb("Bl", [P, D], F32)
        Br = sb("Br", [P, D], F32)
        work = sb("work", [P, 12 * D], F32)

        def wk(n):
            return work[:, n * D:(n + 1) * D]
        agg = work[:, 0:2 * D]
        aggT, act_sum, x1, h2, zs, zT = wk(2), wk(3), wk(4), wk(5), wk(6), wk(7)
        beta_b = act_sum
        stage = work[:, 8 * D:10 * D].bitcast(F16)
        xin = work[:, 10 * D:12 * D]
        t32 = work[:, 0:2 * D]
        dstT = sb("dstT", [P, BC * P], F32)
        srcT = sb("srcT", [P, BC * P], U32)
        idx = sb("idx", [P, 2 * RING], U32)
        iotaf = sb("iotaf", [P, P], F32)
        tile0 = sb("tile0", [P, NT], F32)
        thr = sb("thr", [P, 1], F32)
        ident = sb("ident", [P, P], F32)
        ident16 = sb("ident16", [P, P], F16)
        zero16 = sb("zero16", [P, D], F16)
        onesf = sb("onesf", [P, P], F32)
        last_lane = sb("last_lane", [P, P], F32)
        iota_t = sb("iota_t", [P, P], F32)
        absd = sb("absd", [P, 2 * P], F16)
        eps = sb("eps", [P, 1], F32)
        one_c = sb("one_c", [P, 1], F32)
        gcol = sb("gcol", [P, KC], F32)
        bcol = sb("bcol", [P, KC], F32)
        mv0 = sb("mv0", [P, NT, 2], F32)
        cnt = sb("cnt", [P, NT], F32)
        cols = sb("cols", [P, 10, NT], F32)
        deg, sdeg, dinv, sdx, rstd0, scale0, bias0, dinv_up, cinv_up, has = (cols[:, n, :] for n in range(10))
        be_f = sb("be_f", [P, 2], F32)
        be_c = sb("be_c", [P, 1], F32)
        be_i = sb("be_i", [1, NT + 1], I32)
        st = sb("st", [P, 16], F32)
        mv = sb("mv", [P, 4], F32)
        lnc = sb("lnc", [P, 8], F32)
        natd = sel[:, 0:2 * BC * P].bitcast(I32)
        nats = sel[:, 2 * BC * P:4 * BC * P].bitcast(I32)
        natf = weights[:, 0:2 * BC * P]
        d125 = work[:, 0:HC].bitcast(I32)
        dig_i = work[:, HC:3 * HC].bitcast(I32)
        dig = work[:, 3 * HC:4 * HC].bitcast(F16)
        iotax = weights[:, KC * D:KC * D + DIG * HIST_COLS // 2].bitcast(F16)
        onehot = ring[:, :]
        OH = DIG * HIST_COLS
        stats0 = ring[:, 2 * OH:2 * OH + 12 * NT].bitcast(F32).rearrange("p (t s) -> p t s", s=6)
        hcnt = work[0:NT, 11 * D:11 * D + P]
        wnat = work[:, 4 * HC:4 * HC + 4 * D]

        aggp = ctx.enter_context(nc.psum_tensor("aggp", [P, 2 * 512], F32))
        trp, outp, ztp, misc, misc2 = (bank(n) for n in ("trp", "outp", "ztp", "misc", "misc2"))

        ld_d125, ld_nat, ld_w, ld_small = (sem(n) for n in ("ld_d125", "ld_nat", "ld_w", "ld_small"))
        ld_x = [sem(f"ld_x{g}") for g in range(XG)]
        consts, natz, nat_cast, nat_tr, nat_cp = (sem(n) for n in ("consts", "natz", "nat_cast", "nat_tr", "nat_cp"))
        digits, oh_made, oh_used, hist = (sem(n) for n in ("digits", "oh_made", "oh_used", "hist"))
        dchain, cnt_ok, deg_ok, sdeg_ok, var_ok, sdx_ok, scale_ok = (
            sem(n) for n in ("dchain", "cnt_ok", "deg_ok", "sdeg_ok", "var_ok", "sdx_ok", "scale_ok"))
        bcast, be_ok, be_row, meta = (sem(n) for n in ("bcast", "be_ok", "be_row", "meta"))
        t_made, split0, t1_stored = (sem(n) for n in ("t_made", "split0", "t1_stored"))
        wl_ld, w_tr, w_cp, beta_made, bias_mm, w_done = (
            sem(n) for n in ("wl_ld", "w_tr", "w_cp", "beta_made", "bias_mm", "w_done"))
        got = [[sem(f"got{l}_{j}") for j in range(RING)] for l in range(2)]

        def two(name):
            return [sem(f"{name}{l}") for l in range(2)]
        idx_set, idx_read = two("idx_set"), two("idx_read")
        arrived, freed, s_free, s_ready, s_abs, s_iota = (
            two(n) for n in ("arrived", "freed", "s_free", "s_ready", "s_abs", "s_iota"))
        agg_done, agg_out, agg_tr, aggT_ok, mm_done, mm_read, tin_ld, tin_used, res_ok = (
            two(n) for n in ("agg_done", "agg_out", "agg_tr", "aggT_ok", "mm_done", "mm_read", "tin_ld", "tin_used", "res_ok"))
        v1_ok, sd1_ok, v2_ok, sd2_ok, z_ok, z_tr, zT_ok, split_ok, t2_stored, zT_stored = (
            sem(n) for n in ("v1_ok", "sd1_ok", "v2_ok", "sd2_ok", "z_ok", "z_tr", "zT_ok", "split_ok", "t2_stored", "zT_stored"))
        out_stored = sem("out_stored")
        passed, passed_v = sem("passed"), sem("passed_v")
        vchain = sem("vchain")

        block = ctx.enter_context(nc.Block())

        @block.sync
        def _(sp):
            sp.dma_start(d125[0:HP, :], dst.rearrange("(p c) -> p c", p=HP)).then_inc(ld_d125, 16)
            sp.wait_ge(natz, 2)
            whole = (BC - 1) * P
            for nat, e in ((natd, dst), (nats, src)):
                sp.dma_start(nat[:, 0:whole].rearrange("p (c l) -> p c l", l=P),
                             e[0:whole * P].rearrange("(c p l) -> p c l", p=P, l=P)).then_inc(ld_nat, 16)
                sp.dma_start(nat[0:FULLB - whole, whole:whole + P],
                             e[whole * P:FULLB * P].rearrange("(p l) -> p l", l=P)).then_inc(ld_nat, 16)
                sp.dma_start(nat[FULLB - whole:NB - whole, whole:whole + E - FULLB * P],
                             e[FULLB * P:E].rearrange("(p l) -> p l", p=1)).then_inc(ld_nat, 16)
            sp.dma_start(b0_sb[:, :], b0.rearrange("(a d) -> a d", a=1).broadcast_to((P, D))).then_inc(ld_small, 16)
            sp.dma_start(Br[:, :], b_l.rearrange("(a d) -> a d", a=1).broadcast_to((P, D))).then_inc(ld_small, 16)
            with nc.allow_non_contiguous_dma("512 numbers, once"):
                sp.dma_start(gcol[:, :], gamma.rearrange("(c p) -> p c", p=P)).then_inc(ld_small, 16)
                sp.dma_start(bcol[:, :], beta.rearrange("(c p) -> p c", p=P)).then_inc(ld_small, 16)
            for g in range(XG):
                t0 = g * X_GROUP
                n = X_GROUP if g < XG - 1 else X_GROUP - 1
                sp.dma_start(nodes[:, t0 * D:(t0 + n) * D].rearrange("p (t d) -> p t d", d=D),
                             x[t0 * P:(t0 + n) * P, :].rearrange("(t p) d -> p t d", p=P)).then_inc(ld_x[g], 16)
                if g == XG - 1:
                    sp.wait_ge(consts, 1)
                    sp.dma_start(nodes[0:LAST, (NT - 1) * D:NT * D], x[(NT - 1) * P:N, :]).then_inc(ld_x[g], 16)
            sp.wait_ge(hist, 1)
            sp.dma_start(w0_sb[:, :].rearrange("p (c n) -> p c n", n=D),
                         W0.rearrange("(c p) n -> p c n", p=P)).then_inc(ld_w, 16)
            for n, w in enumerate((w_l, w_r)):
                if n == 1:
                    sp.wait_ge(w_tr, KC)
                sp.dma_start(wnat.rearrange("p (c n) -> p c n", n=D),
                             w.rearrange("(c p) n -> p c n", p=P)).then_inc(wl_ld, 16)
            for g in range(XG):
                sp.wait_ge(split0, X_GROUP * (g + 1))
                t0 = g * X_GROUP
                sp.dma_start(table[0][t0 * P:(t0 + X_GROUP) * P, :].rearrange("(t p) c -> p t c", p=P),
                             nodes16[:, t0 * 2 * D:(t0 + X_GROUP) * 2 * D].rearrange("p (t c) -> p t c", c=2 * D)
                             ).then_inc(t1_stored, 16)
            for l in range(2):
                with sp.Fori(0, GROUPS) as g:
                    for j in range(RING):
                        sp.wait_ge(got[l][j], g * 16 + 16)
                        sp.sem_inc(arrived[l], 1)

        @block.gpsimd
        def _(pool):
            pool.memset(natd, -1).then_inc(natz, 1)
            pool.memset(nats, 0).then_inc(natz, 1)
            pool.iota(iotax[:, 0:NT * HIST_COLS], [[1, NT], [0, HIST_COLS]], base=0, channel_multiplier=0,
                      allow_small_or_imprecise_dtypes=True).then_inc(digits, 1)
            pool.iota(iotax[:, NT * HIST_COLS:], [[1, P], [0, HIST_COLS]], base=0, channel_multiplier=0,
                      allow_small_or_imprecise_dtypes=True).then_inc(digits, 1)
            pool.memset(nodes[:, (NT - 1) * D:NT * D], 0.0).then_inc(consts, 1)
            for t, v in ((ident, 0.0), (ident16, 0.0), (zero16, 0.0), (onesf, 1.0), (last_lane, 1.0), (eps, EPS), (one_c, 1.0)):
                pool.memset(t[:, :], v).then_inc(consts, 1)
            pool.iota(iotaf[:, :], [[1, P]], base=0, channel_multiplier=0,
                      allow_small_or_imprecise_dtypes=True).then_inc(consts, 1)
            pool.iota(tile0[:, :], [[P, NT]], base=0, channel_multiplier=0,
                      allow_small_or_imprecise_dtypes=True).then_inc(consts, 1)
            pool.iota(thr[:, :], [[0, 1]], base=P, channel_multiplier=P,
                      allow_small_or_imprecise_dtypes=True).then_inc(consts, 1)
            pool.wait_ge(consts, 11)
            for m in (ident, ident16):
                pool.affine_select(out=m[:, :], in_=m[:, :], compare_op=ALU.not_equal, fill=1.0,
                                   base=0, pattern=[[-1, P]], channel_multiplier=1).then_inc(consts, 1)
            pool.affine_select(out=last_lane[:, :], in_=last_lane[:, :], compare_op=ALU.is_ge, fill=0.0,
                               base=-(P - 1), pattern=[[0, P]], channel_multiplier=1).then_inc(consts, 1)
            for l in range(2):
                if l == 0:
                    pool.wait_ge(t1_stored, 16 * XG)
                    pool.wait_ge(meta, 2)
                else:
                    pool.wait_ge(t2_stored, 16 * NT)
                    pool.wait_ge(arrived[0], GROUPS * RING)
                    pool.wait_ge(s_free[0], STEPS + SRING)
                pool.sem_inc(freed[l], RING)

                def gather_round(g, q):
                    for j in range(RING):
                        if j % WAIT_EVERY == 0:
                            pool.wait_ge(freed[l], g * RING + (j + WAIT_EVERY))
                            pool.sem_inc(passed, 1)
                        if j == 0:
                            pool.tensor_copy(idx[:, q * RING:(q + 1) * RING], srcT[:, ds(g * RING, RING)]).then_inc(idx_set[l], 1)
                            pool.wait_ge(idx_set[l], g + 1)
                            pool.sem_inc(passed, 1)
                        c = q * RING + j
                        pool.indirect_dma_start(
                            out=ring[:, j * 2 * D:(j + 1) * 2 * D], out_offset=None, in_=table[l],
                            in_offset=bass.IndirectOffsetOnAxis(ap=idx[:, c:c + 1], axis=0)).then_inc(got[l][j], 16)

                assert GROUPS % 2 == 1
                with pool.Fori(0, GROUPS - 1, 2) as g:
                    gather_round(g, 0)
                    gather_round(g + 1, 1)
                gather_round(GROUPS - 1, 0)

        def selection(act, l, T):
            lo = act.value_load(be_i[0:1, ds(T, 1)], min_val=0, max_val=NB - 1)
            hi = act.value_load(be_i[0:1, ds(T + 1, 1)], min_val=0, max_val=NB - 1)
            nc.scalar.activation(iota_t[:, :], iotaf[:, :], ACT.Identity, bias=tile0[:, ds(T, 1)]).then_inc(s_iota[l], 1)
            act.wait_ge(s_iota[l], T + 1)
            with act.Fori(lo, hi + 1) as b:
                act.wait_ge(s_free[l], b + T + 1)
                ad = absd[:, ds(((b + T) % 2) * P, P)]
                nc.scalar.activation(ad, iota_t[:, :], ACT.Abs, bias=dstT[:, ds(b, 1)], scale=-1.0).then_inc(s_abs[l], 1)
                act.wait_ge(s_abs[l], b + T + 1)
                nc.scalar.activation(sel[:, ds(((b + T) % SRING) * P, P)], ad, ACT.Relu,
                                     bias=one_c[:, :], scale=-1.0).then_inc(s_ready[l], 1)

        @block.scalar
        def _(act):
            act.wait_ge(consts, 14)
            for n, w in enumerate((wl_sb, wr_sb)):
                for c in range(KC):
                    act.wait_ge(w_tr, n * KC + c + 1)
                    if n == 0 and c == 0:
                        act.wait_ge(nat_tr, 2 * BC)
                    nc.scalar.activation(w[:, c * D:(c + 1) * D], ztp[:, :], ACT.Copy).then_inc(w_cp, 1)
            act.wait_ge(deg_ok, 1)
            nc.scalar.activation(sdeg, deg, ACT.Sqrt).then_inc(sdeg_ok, 1)
            act.wait_ge(var_ok, NT)
            nc.scalar.activation(sdx, mv0[:, :, 1], ACT.Sqrt, bias=eps[:, :]).then_inc(sdx_ok, 1)
            act.wait_ge(scale_ok, 1)
            def scaled(T, q):
                nc.scalar.activation(t32[:, q * D:(q + 1) * D], nodes[:, ds(T * D, D)], ACT.Relu,
                                     bias=bias0[:, ds(T, 1)], scale=scale0[:, ds(T, 1)]).then_inc(t_made, 1)

            scaled(0, 0)
            scaled(1, 1)
            with act.Fori(2, NT - 1, 2) as T:
                for q in range(2):
                    act.wait_ge(split0, T + q - 1)
                    scaled(T + q, q)
            act.wait_ge(split0, NT - 2)
            scaled(NT - 1, 0)

            def load_x(T, rows):
                act.dma_start(xin[0:rows, ds((T % 2) * D, D)], x[ds(T * P, rows), :]).then_inc(tin_ld[0], 16)

            def norms(T):
                act.wait_ge(v1_ok, T + 1)
                nc.scalar.activation(lnc[:, 0:1], mv[:, 1:2], ACT.Sqrt, bias=eps[:, :]).then_inc(sd1_ok, 1)
                act.wait_ge(v2_ok, T + 1)
                nc.scalar.activation(lnc[:, 4:5], mv[:, 3:4], ACT.Sqrt, bias=eps[:, :]).then_inc(sd2_ok, 1)

            def store_table(T, first=False):
                act.wait_ge(split_ok, T + 1)
                if not first:
                    act.wait_ge(t2_stored, T * 16)
                act.dma_start(table[1][ds(T * P, P), :], stage[:, ds((T % 2) * 2 * D, 2 * D)]).then_inc(t2_stored, 16)

            def store_zT(T, first=False):
                act.wait_ge(zT_ok, T + 1)
                if not first:
                    act.wait_ge(zT_stored, T * 16)
                act.dma_start(xT_dram[ds(T * P, P), :], zT).then_inc(zT_stored, 16)

            act.wait_ge(be_row, 2)
            act.wait_ge(split0, NT)
            act.sem_inc(s_free[0], SRING)
            load_x(0, P)
            selection(act, 0, 0)
            act.wait_ge(tin_ld[0], 16)
            load_x(1, P)
            selection(act, 0, 1)
            for T in (2, 3):
                selection(act, 0, T)
                norms(T - 2)
                store_table(T - 2, first=(T == 2))
                if T == 3:
                    store_zT(0, first=True)
                act.wait_ge(tin_used[0], T - 1)
                act.wait_ge(tin_ld[0], 16 * T)
                load_x(T, P)
            with act.Fori(4, NT - 1) as T:
                selection(act, 0, T)
                norms(T - 2)
                store_table(T - 2)
                store_zT(T - 3)
                act.wait_ge(tin_used[0], T - 1)
                act.wait_ge(tin_ld[0], T * 16)
                load_x(T, P)
            for T in range(NT - 1, NT + 2):
                if T < NT:
                    selection(act, 0, T)
                if T - 2 < NT:
                    norms(T - 2)
                    store_table(T - 2)
                store_zT(T - 3)
                if T == NT - 1:
                    act.wait_ge(tin_used[0], T - 1)
                    act.wait_ge(tin_ld[0], T * 16)
                    load_x(T, LAST)
            store_zT(NT - 1)
            act.wait_ge(zT_stored, 16 * NT)

            def load_xT(T):
                act.dma_start(xin[:, ds((T % 2) * D, D)], xT_dram[ds(T * P, P), :]).then_inc(tin_ld[1], 16)

            def store_out(T, rows, first=False):
                act.wait_ge(res_ok[1], T + 1)
                if not first:
                    act.wait_ge(out_stored, T * 16)
                act.dma_start(out[ds(T * P, rows), :], agg_o[0:rows, ds((T % 2) * D, D)]).then_inc(out_stored, 16)

            agg_o = stage.bitcast(F32)
            act.wait_ge(s_free[0], STEPS + SRING)
            act.sem_inc(s_free[1], SRING)
            act.wait_ge(tin_used[0], NT)
            load_xT(0)
            selection(act, 1, 0)
            act.wait_ge(tin_ld[1], 16)
            load_xT(1)
            selection(act, 1, 1)
            for T in (2,):
                selection(act, 1, T)
                store_out(T - 2, P, first=True)
                act.wait_ge(tin_used[1], T - 1)
                act.wait_ge(tin_ld[1], T * 16)
                load_xT(T)
            with act.Fori(3, NT) as T:
                selection(act, 1, T)
                store_out(T - 2, P)
                act.wait_ge(tin_used[1], T - 1)
                act.wait_ge(tin_ld[1], T * 16)
                load_xT(T)
            store_out(NT - 2, P)
            store_out(NT - 1, LAST)
            act.wait_ge(out_stored, 16 * NT)

        @block.tensor
        def _(pe):
            pe.wait_ge(consts, 14)
            pe.wait_ge(nat_cast, 2)
            for k in range(2 * BC):
                bk = (misc, misc2)[k % 2]
                if k >= 2:
                    pe.wait_ge(nat_cp, k - 1)
                pe.transpose(bk[:, 0:P], natf[:, k * P:(k + 1) * P], ident[:, :]).then_inc(nat_tr, 1)
            pe.wait_ge(nat_cp, 2 * BC)
            half = NB // 2
            for k, bk in enumerate((outp, trp)):
                pe.matmul(bk[:, 0:half], last_lane[:, :], dstT[:, k * half:(k + 1) * half],
                          start=True, stop=True).then_inc(bcast, 1)
            pe.wait_ge(meta, 1)
            for k in range(CHUNKS):
                pe.wait_ge(oh_made, k + 1)
                o = (k % 2) * OH
                v = onehot[0:HP, o:o + OH].rearrange("p (v c) -> p v c", c=HIST_COLS)
                for c in range(HIST_COLS):
                    mm = pe.matmul(misc[0:NT, 0:P], v[:, 0:NT, c], v[:, NT:DIG, c],
                                   start=(k == 0 and c == 0), stop=(k == CHUNKS - 1 and c == HIST_COLS - 1))
                mm.then_inc(oh_used, 1)
            pe.wait_ge(hist, 1)
            pe.transpose(misc2[:, 0:NT], hcnt, ident[0:NT, 0:NT]).then_inc(cnt_ok, 1)
            pe.wait_ge(be_ok, 3)
            pe.matmul(misc[0:1, 0:NT], be_c[0:NT, :], ident[0:NT, 0:NT], start=True, stop=True,
                      skip_group_check=True).then_inc(be_row, 1)
            for n in range(2):
                pe.wait_ge(wl_ld, 16 * (n + 1))
                for c in range(KC):
                    if n or c:
                        pe.wait_ge(w_cp, n * KC + c)
                    for r in range(KC):
                        mm = pe.transpose(ztp[:, r * P:(r + 1) * P], wnat[:, r * D + c * P:r * D + (c + 1) * P], ident[:, :])
                    mm.then_inc(w_tr, 1)
            pe.wait_ge(beta_made, KC)
            pe.wait_ge(w_cp, 2 * KC)
            for w, bk in ((wl_sb, outp), (wr_sb, trp)):
                for c in range(KC):
                    mm = pe.matmul(bk[:, :], beta_b[:, c * P:(c + 1) * P], w[:, c * D:(c + 1) * D],
                                   start=(c == 0), stop=(c == KC - 1))
                mm.then_inc(bias_mm, 1)
            pe.wait_ge(ld_w, 16)
            pe.wait_ge(split0, NT)

            def gathered(l, T, q):
                a = aggp[:, q * 512:(q + 1) * 512]
                lo = pe.value_load(be_i[0:1, ds(T, 1)], min_val=0, max_val=NB - 1)
                hi = pe.value_load(be_i[0:1, ds(T + 1, 1)], min_val=0, max_val=NB - 1)

                if not isinstance(T, int) or T >= 2:
                    pe.wait_ge(agg_out[l], T - 1)

                def step(b, first):
                    pe.wait_ge(arrived[l], b + 1)
                    pe.wait_ge(s_ready[l], b + T + 1)
                    s = sel[:, ds(((b + T) % SRING) * P, P)]
                    r = (b % RING) * (2 * D)
                    mm = pe.matmul(a, s, ring[:, ds(r, D)], start=first, stop=False, skip_group_check=True)
                    if not first:
                        mm.then_inc(freed[l], 1)
                    pe.matmul(a, s, ring[:, ds(r + D, D)], start=False, stop=False,
                              skip_group_check=True).then_inc(s_free[l], 1)

                step(lo, True)
                with pe.If(lo < hi):
                    with pe.Fori(lo + 1, hi + 1) as b:
                        step(b, False)
                if l == 0:
                    pe.matmul(a, ident16[:, :], nodes16[:, ds(T * 2 * D, D)], start=False, stop=False, skip_group_check=True)
                    mm = pe.matmul(a, ident16[:, :], nodes16[:, ds(T * 2 * D + D, D)], start=False, stop=True,
                                   skip_group_check=True)
                else:
                    mm = pe.matmul(a, ident16[:, :], zero16[:, :], start=False, stop=True, skip_group_check=True)
                mm.then_inc(agg_done[l], 1)

            def turn_agg(l, T, q):
                pe.wait_ge(agg_out[l], T + 1)
                if not isinstance(T, int) or T:
                    pe.wait_ge(aggT_ok[l], T)
                for c in range(KC):
                    mm = pe.transpose(trp[:, c * P:(c + 1) * P], agg[:, q * D + c * P:q * D + (c + 1) * P], ident[:, :])
                mm.then_inc(agg_tr[l], 1)

            def project(l, T, q, w, more=None):
                pe.wait_ge(aggT_ok[l], T + 1)
                if not isinstance(T, int) or T:
                    pe.wait_ge(mm_read[l], T)
                for c in range(KC):
                    mm = pe.matmul(outp[:, :], aggT[:, c * P:(c + 1) * P], w[:, c * D:(c + 1) * D],
                                   start=(c == 0), stop=(c == KC - 1 and more is None))
                if more is not None:
                    pe.wait_ge(tin_ld[l], T * 16 + 16)
                    for c in range(KC):
                        mm = pe.matmul(outp[:, :], xin[:, q * D + c * P:q * D + (c + 1) * P], more[:, c * D:(c + 1) * D],
                                       start=False, stop=(c == KC - 1))
                mm.then_inc(mm_done[l], 1)

            def turn_z(T):
                pe.wait_ge(split_ok, T + 1)
                if not isinstance(T, int) or T:
                    pe.wait_ge(zT_ok, T)
                for c in range(KC):
                    mm = pe.transpose(ztp[:, c * P:(c + 1) * P], zs[:, c * P:(c + 1) * P], ident[:, :])
                mm.then_inc(z_tr, 1)

            def first_phase(T, q):
                gathered(0, T, q)
                if not isinstance(T, int) or T >= 1:
                    turn_agg(0, T - 1, 1 - q)
                if not isinstance(T, int) or T >= 2:
                    turn_z(T - 2)
                if not isinstance(T, int) or T >= 1:
                    project(0, T - 1, 1 - q, w0_sb)

            def second_phase(T, q):
                gathered(1, T, q)
                if not isinstance(T, int) or T >= 1:
                    turn_agg(1, T - 1, 1 - q)
                    project(1, T - 1, 1 - q, wl_sb, wr_sb)

            first_phase(0, 0)
            first_phase(1, 1)
            with pe.Fori(2, NT - 1, 2) as T:
                first_phase(T, 0)
                first_phase(T + 1, 1)
            first_phase(NT - 1, 0)
            turn_agg(0, NT - 1, 0)
            turn_z(NT - 2)
            project(0, NT - 1, 0, w0_sb)
            turn_z(NT - 1)

            pe.wait_ge(agg_out[0], NT)
            pe.wait_ge(w_done, 2 * KC)
            second_phase(0, 0)
            second_phase(1, 1)
            with pe.Fori(2, NT - 1, 2) as T:
                second_phase(T, 0)
                second_phase(T + 1, 1)
            second_phase(NT - 1, 0)
            turn_agg(1, NT - 1, 0)
            project(1, NT - 1, 0, wl_sb, wr_sb)

        @block.vector
        def _(dve):
            v = nc.vector
            link_n = [0]

            def link(ins, sem_=dchain):
                link_n[0] += 1
                ins.then_inc(dchain, 1)
                dve.wait_ge(dchain, link_n[0])

            dve.wait_ge(ld_nat, 96)
            v.tensor_copy(natf[:, 0:BC * P], natd).then_inc(nat_cast, 1)
            v.tensor_copy(natf[:, BC * P:2 * BC * P], nats).then_inc(nat_cast, 1)
            for k in range(2 * BC):
                bk = (misc, misc2)[k % 2]
                dve.wait_ge(nat_tr, k + 1)
                to = dstT if k < BC else srcT
                v.tensor_copy(to[:, (k % BC) * P:(k % BC + 1) * P], bk[:, 0:P]).then_inc(nat_cp, 1)
            dve.wait_ge(nat_cp, 2 * BC)
            v.memset(be_i[0:1, 0:1], 0).then_inc(meta, 1)
            v.memset(be_c[:, :], 0.0).then_inc(meta, 1)
            dve.wait_ge(ld_d125, 16)
            v.tensor_scalar(dig_i[0:HP, 0:HC], d125[0:HP, :], 7, None, ALU.arith_shift_right).then_inc(digits, 1)
            v.tensor_scalar(dig_i[0:HP, HC:2 * HC], d125[0:HP, :], P - 1, None, ALU.bitwise_and).then_inc(digits, 1)
            dve.wait_ge(digits, 4)
            v.tensor_copy(dig[0:HP, :], dig_i[0:HP, :]).then_inc(digits, 1)
            dve.wait_ge(digits, 5)
            for k in range(CHUNKS):
                if k >= 2:
                    dve.wait_ge(oh_used, k - 1)
                o = (k % 2) * OH
                for a, n, d0 in ((0, NT, 0), (NT, P, HC)):
                    ins = v.tensor_tensor(
                        onehot[0:HP, o + a * HIST_COLS:o + (a + n) * HIST_COLS].rearrange("p (v c) -> p v c", c=HIST_COLS),
                        dig[0:HP, d0 + k * HIST_COLS:d0 + (k + 1) * HIST_COLS].rearrange("p (a c) -> p a c", a=1).broadcast_to((HP, n, HIST_COLS)),
                        iotax[0:HP, a * HIST_COLS:(a + n) * HIST_COLS].rearrange("p (v c) -> p v c", c=HIST_COLS),
                        ALU.is_equal)
                ins.then_inc(oh_made, 1)
            dve.wait_ge(oh_used, CHUNKS)
            v.tensor_copy(hcnt, misc[0:NT, 0:P]).then_inc(hist, 1)
            half = NB // 2
            dve.wait_ge(bcast, 2)
            v.tensor_scalar(act_sum[:, 0:half], outp[:, 0:half], thr[:, :], 0.0, ALU.is_lt, ALU.add,
                            accum_out=be_f[:, 0:1]).then_inc(be_ok, 1)
            v.tensor_scalar(x1[:, 0:half - 1], trp[:, 0:half - 1], thr[:, :], 0.0, ALU.is_lt, ALU.add,
                            accum_out=be_f[:, 1:2]).then_inc(be_ok, 1)
            dve.wait_ge(be_ok, 2)
            v.tensor_tensor(be_c[:, :], be_f[:, 0:1], be_f[:, 1:2], ALU.add).then_inc(be_ok, 1)
            dve.wait_ge(cnt_ok, 1)
            link(v.tensor_copy(cnt[:, :], misc2[:, 0:NT]))
            v.tensor_scalar(deg, cnt[:, :], 1.0, None, ALU.add).then_inc(deg_ok, 1)
            dve.wait_ge(be_row, 1)
            v.tensor_copy(be_i[0:1, 1:NT + 1], misc[0:1, 0:NT]).then_inc(be_row, 1)
            link(v.tensor_scalar(has, cnt[:, :], 1.0, None, ALU.min))
            link(v.tensor_scalar(cinv_up, cnt[:, :], 1.0, None, ALU.max))
            link(v.reciprocal(cinv_up, cinv_up))
            link(v.tensor_scalar(cinv_up, cinv_up, 1.0 / UP, None, ALU.mult))
            dve.wait_ge(ld_small, 64)
            for c in range(KC):
                v.tensor_scalar(beta_b[:, c * P:(c + 1) * P], onesf[:, :], bcol[:, c:c + 1], None,
                                ALU.mult).then_inc(beta_made, 1)
            for T in range(NT):
                if T % X_GROUP == 0:
                    g = T // X_GROUP
                    dve.wait_ge(ld_x[g], 32 if g == XG - 1 else 16)
                link(v.bn_stats(stats0[:, T, :], nodes[:, T * D:(T + 1) * D]))
                v.bn_aggr(mv0[:, T, :], stats0[:, T, :]).then_inc(var_ok, 1)
            dve.wait_ge(sdeg_ok, 1)
            link(v.reciprocal(dinv, sdeg))
            link(v.tensor_scalar(dinv_up, dinv, 1.0 / UP, None, ALU.mult))
            dve.wait_ge(sdx_ok, 1)
            link(v.reciprocal(rstd0, sdx))
            link(v.tensor_tensor(scale0, rstd0, dinv, ALU.mult))
            link(v.tensor_scalar(scale0, scale0, UP, None, ALU.mult))
            v.scalar_tensor_tensor(bias0, mv0[:, :, 0], -1.0, scale0, ALU.mult, ALU.mult).then_inc(scale_ok, 1)
            with dve.Fori(0, NT) as T:
                dve.wait_ge(t_made, T + 1)
                t = t32[:, ds((T % 2) * D, D)]
                v.tensor_copy(nodes16[:, ds(T * 2 * D, D)], t).then_inc(vchain, 1)
                dve.wait_ge(vchain, T + 1)
                v.tensor_tensor(nodes16[:, ds(T * 2 * D + D, D)], t, nodes16[:, ds(T * 2 * D, D)],
                                ALU.subtract).then_inc(split0, 1)
            dve.wait_ge(bias_mm, 2)
            link(v.tensor_copy(Bl[:, :], outp[:, :]))
            link(v.tensor_tensor(Br[:, :], trp[:, :], Br[:, :], ALU.add))
            for w, up in ((wl_sb, 1.0), (wr_sb, 1.0 / UP)):
                for c in range(KC):
                    v.tensor_scalar(w[:, c * D:(c + 1) * D], w[:, c * D:(c + 1) * D], gcol[:, c:c + 1], up,
                                    ALU.mult, ALU.mult).then_inc(w_done, 1)

            def evacuate(l, T, by):
                dve.wait_ge(agg_done[l], T + 1)
                if not isinstance(T, int) or T >= 2:
                    dve.wait_ge(agg_tr[l], T - 1)
                v.tensor_scalar(agg[:, ds((T % 2) * D, D)], aggp[:, ds((T % 2) * 512, 512)], by[:, ds(T, 1)], None,
                                ALU.mult).then_inc(agg_out[l], 1)

            def copy_aggT(l, T):
                dve.wait_ge(agg_tr[l], T + 1)
                if not isinstance(T, int) or T:
                    dve.wait_ge(mm_done[l], T)
                v.tensor_copy(aggT, trp[:, :]).then_inc(aggT_ok[l], 1)

            def copy_zT(T):
                dve.wait_ge(z_tr, T + 1)
                if not isinstance(T, int) or T:
                    dve.wait_ge(zT_stored, T * 16)
                v.tensor_copy(zT, ztp[:, :]).then_inc(zT_ok, 1)

            LINKS = 10

            def chain0(T):
                n = [0]

                def then(ins):
                    n[0] += 1
                    ins.then_inc(v0, 1)
                    dve.wait_ge(v0, T * LINKS + n[0])
                dve.wait_ge(mm_done[0], T + 1)
                ins = v.tensor_tensor(act_sum, outp[:, :], b0_sb[:, :], ALU.add)
                ins.then_inc(mm_read[0], 1)
                dve.wait_ge(mm_read[0], T + 1)
                dve.wait_ge(tin_ld[0], T * 16 + 16)
                v.scalar_tensor_tensor(x1, act_sum, 0.0, xin[:, ds((T % 2) * D, D)], ALU.max, ALU.add).then_inc(tin_used[0], 1)
                dve.wait_ge(tin_used[0], T + 1)
                then(v.bn_stats(st[:, 0:6], x1))
                dve.sem_inc(passed_v, 1)
                v.bn_aggr(mv[:, 0:2], st[:, 0:6]).then_inc(v1_ok, 1)
                dve.wait_ge(v1_ok, T + 1)
                dve.wait_ge(sd1_ok, T + 1)
                then(v.reciprocal(lnc[:, 1:2], lnc[:, 0:1]))
                then(v.scalar_tensor_tensor(lnc[:, 2:3], mv[:, 0:1], -1.0, lnc[:, 1:2], ALU.mult, ALU.mult))
                then(v.tensor_scalar(h2, x1, lnc[:, 1:2], lnc[:, 2:3], ALU.mult, ALU.add))
                then(v.tensor_scalar(h2, h2, 0.0, None, ALU.max))
                then(v.bn_stats(st[:, 6:12], h2))
                dve.sem_inc(passed_v, 1)
                v.bn_aggr(mv[:, 2:4], st[:, 6:12]).then_inc(v2_ok, 1)
                dve.wait_ge(sd2_ok, T + 1)
                then(v.reciprocal(lnc[:, 5:6], lnc[:, 4:5]))
                then(v.tensor_scalar(lnc[:, 5:6], lnc[:, 5:6], UP, None, ALU.mult))
                then(v.tensor_scalar(zs, h2, mv[:, 2:3], lnc[:, 5:6], ALU.subtract, ALU.mult))
                v.tensor_tensor(nodes[:, ds(T * D, D)], x1, h2, ALU.add).then_inc(res_ok[0], 1)
                dve.wait_ge(res_ok[0], T + 1)
                if not isinstance(T, int) or T >= 2:
                    dve.wait_ge(t2_stored, (T - 1) * 16)
                s = (T % 2) * (2 * D)
                then(v.tensor_copy(stage[:, ds(s, D)], zs))
                v.tensor_tensor(stage[:, ds(s + D, D)], zs, stage[:, ds(s, D)], ALU.subtract).then_inc(split_ok, 1)
                assert n[0] == LINKS

            v0 = sem("v0")
            evacuate(0, 0, dinv_up)
            evacuate(0, 1, dinv_up)
            copy_aggT(0, 0)
            chain0(0)
            with dve.Fori(2, NT) as T:
                evacuate(0, T, dinv_up)
                copy_aggT(0, T - 1)
                copy_zT(T - 2)
                chain0(T - 1)
            copy_aggT(0, NT - 1)
            copy_zT(NT - 2)
            chain0(NT - 1)
            copy_zT(NT - 1)

            res = stage.bitcast(F32)

            def chain1(T):
                dve.wait_ge(mm_done[1], T + 1)
                v.scalar_tensor_tensor(act_sum, Bl[:, :], has[:, ds(T, 1)], outp[:, :], ALU.mult, ALU.add).then_inc(mm_read[1], 1)
                dve.wait_ge(mm_read[1], T + 1)
                v.tensor_tensor(x1, act_sum, Br[:, :], ALU.add).then_inc(tin_used[1], 1)
                dve.wait_ge(tin_used[1], T + 1)
                if not isinstance(T, int) or T >= 2:
                    dve.wait_ge(out_stored, (T - 1) * 16)
                else:
                    dve.wait_ge(t2_stored, NT * 16)
                v.scalar_tensor_tensor(res[:, ds((T % 2) * D, D)], x1, 0.0, nodes[:, ds(T * D, D)], ALU.max,
                                       ALU.add).then_inc(res_ok[1], 1)

            evacuate(1, 0, cinv_up)
            evacuate(1, 1, cinv_up)
            copy_aggT(1, 0)
            chain1(0)
            evacuate(1, 2, cinv_up)
            copy_aggT(1, 1)
            chain1(1)
            with dve.Fori(3, NT) as T:
                evacuate(1, T, cinv_up)
                copy_aggT(1, T - 1)
                chain1(T - 1)
            copy_aggT(1, NT - 1)
            chain1(NT - 1)


_INS = ['x', 'src', 'dst', 'L0_gnn_W', 'L0_gnn_b', 'L1_gnn_ln_gamma', 'L1_gnn_ln_beta', 'L1_gnn_w_l', 'L1_gnn_b_l', 'L1_gnn_w_r']


def kernel(**inputs):
    import numpy as _np
    import concourse.bacc as _bacc
    from concourse import mybir as _mybir
    from concourse.bass_utils import run_bass_kernel_spmd as _run

    nc = _bacc.Bacc("TRN2", target_bir_lowering=False, num_devices=1)
    arrays, args = {}, []
    for name in _INS:
        a = _np.ascontiguousarray(inputs[name])
        arrays[f"in_{name}_dram"] = a
        args.append(nc.dram_tensor(f"in_{name}_dram", a.shape, _mybir.dt.from_np(a.dtype), kind="ExternalInput").ap())
    shape = inputs['x'].shape
    out = nc.dram_tensor("out_0_dram", shape, _mybir.dt.float32, kind="ExternalOutput").ap()
    gnn_kernel(nc, *args, out)
    r = _run(nc, [arrays], core_ids=[0])
    return r.results[0]["out_0_dram"]
```

```python
from contextlib import ExitStack

import concourse.bass as bass
from concourse import mybir

ALU = mybir.AluOpType
ACT = mybir.ActivationFunctionType
F32 = mybir.dt.float32
F16 = mybir.dt.float16
I32 = mybir.dt.int32
U32 = mybir.dt.uint32

P = 128
QUAD = 4
RING = 16
RQ = RING // QUAD
SQ = 8
EPS = 1e-5
UP = 2048.0
HIST_COLS = 40
X_GROUP = 7


def ds(start, size):
    return bass.ds(start, size)


def gnn_kernel(nc, x, src, dst, W0, b0, gamma, beta, w_l, b_l, w_r, out):
    N, D = x.shape
    E = src.shape[0]
    KC = D // P
    NT = (N + P - 1) // P
    LAST = N - (NT - 1) * P
    NB = (E + P - 1) // P
    FULLB = E // P
    BC = (NB + P - 1) // P
    NQ = (NB + QUAD - 1) // QUAD
    STEPS = NQ + NT - 1
    GROUPS = (NB + RING - 1) // RING
    HP = 125
    HC = E // HP
    CHUNKS = HC // HIST_COLS
    XG = NT // X_GROUP
    DIG = NT + P
    assert HP * HC == E and CHUNKS * HIST_COLS == HC and XG * X_GROUP == NT and D == 512

    table = [nc.dram_tensor(f"table{n}", [NT * P, 2 * D], F16, kind="Internal").ap() for n in range(2)]
    xT_dram = nc.dram_tensor("xT_dram", [NT * P, D], F32, kind="Internal").ap()

    with ExitStack() as ctx:
        def sb(name, shape, dt):
            return ctx.enter_context(nc.sbuf_tensor(name, shape, dt))

        def bank(name):
            return ctx.enter_context(nc.psum_tensor(name, [P, 512], F32))

        def sem(name):
            return ctx.enter_context(nc.semaphore(name))

        nodes = sb("nodes", [P, NT * D], F32)
        nodes16 = nodes[:, :].bitcast(F16)
        ring = sb("ring", [P, RING * 2 * D], F16)
        sel = sb("sel", [P, SQ * QUAD * P], F16)
        weights = sb("weights", [P, 3 * KC * D], F32)
        w0_sb, wl_sb, wr_sb = (weights[:, n * KC * D:(n + 1) * KC * D] for n in range(3))
        b0_sb = sb("b0_sb", [P, D], F32)
        Bl = sb("Bl", [P, D], F32)
        Br = sb("Br", [P, D], F32)
        work = sb("work", [P, 12 * D], F32)

        def wk(n):
            return work[:, n * D:(n + 1) * D]
        agg = work[:, 0:2 * D]
        aggT, act_sum, x1, g1, zs, zT = wk(2), wk(3), wk(4), wk(5), wk(6), wk(7)
        beta_b = act_sum
        stage = work[:, 8 * D:10 * D].bitcast(F16)
        res = work[:, 8 * D:10 * D]
        xin = work[:, 10 * D:12 * D]
        t32 = work[:, 0:2 * D]
        dstT = sb("dstT", [P, NQ * QUAD], F32)
        srcT = sb("srcT", [P, NQ * QUAD], U32)
        idx = sb("idx", [P, 2 * RING], U32)
        iotaf = sb("iotaf", [P, P], F32)
        tile0 = sb("tile0", [P, NT], F32)
        thr = sb("thr", [P, 1], F32)
        ident = sb("ident", [P, P], F32)
        ident16 = sb("ident16", [P, P], F16)
        zero16 = sb("zero16", [P, D], F16)
        onesf = sb("onesf", [P, P], F32)
        last_lane = sb("last_lane", [P, P], F32)
        iota_t = sb("iota_t", [P, P], F32)
        absd = sb("absd", [P, 2 * QUAD * P], F16)
        eps = sb("eps", [P, 1], F32)
        one_c = sb("one_c", [P, 1], F32)
        gcol = sb("gcol", [P, KC], F32)
        bcol = sb("bcol", [P, KC], F32)
        mv0 = sb("mv0", [P, NT, 2], F32)
        cnt = sb("cnt", [P, NT], F32)
        cols = sb("cols", [P, 10, NT], F32)
        deg, sdeg, dinv, sdx, rstd0, scale0, bias0, dinv_up, cinv_up, has = (cols[:, n, :] for n in range(10))
        be_c = sb("be_c", [P, 1], F32)
        be_i = sb("be_i", [1, NT + 1], I32)
        st = sb("st", [P, 12], F32)
        mv = sb("mv", [P, 4], F32)
        rs = sb("rs", [P, 12], F32)
        natd = sel[:, 0:2 * BC * P].bitcast(I32)
        nats = sel[:, 2 * BC * P:4 * BC * P].bitcast(I32)
        natf = weights[:, 0:2 * BC * P]
        d125 = work[:, 0:HC].bitcast(I32)
        dig_i = work[:, HC:3 * HC].bitcast(I32)
        dig = work[:, 3 * HC:4 * HC].bitcast(F16)
        iotax = weights[:, KC * D:KC * D + DIG * HIST_COLS // 2].bitcast(F16)
        onehot = ring[:, :]
        OH = DIG * HIST_COLS
        stats0 = ring[:, 2 * OH:2 * OH + 12 * NT].bitcast(F32).rearrange("p (t s) -> p t s", s=6)
        hcnt = work[0:NT, 11 * D:11 * D + P]
        wnat = work[:, 4 * HC:4 * HC + 4 * D]

        aggp = ctx.enter_context(nc.psum_tensor("aggp", [P, 2 * 512], F32))
        trp, outp, ztp, misc, misc2 = (bank(n) for n in ("trp", "outp", "ztp", "misc", "misc2"))

        ld_d125, ld_nat, ld_w, ld_small = (sem(n) for n in ("ld_d125", "ld_nat", "ld_w", "ld_small"))
        ld_x = [sem(f"ld_x{g}") for g in range(XG)]
        consts, natz, nat_cast, nat_tr, nat_cp = (sem(n) for n in ("consts", "natz", "nat_cast", "nat_tr", "nat_cp"))
        digits, oh_made, oh_used, hist = (sem(n) for n in ("digits", "oh_made", "oh_used", "hist"))
        dchain, cnt_ok, deg_ok, sdeg_ok, var_ok, sdx_ok, scale_ok = (
            sem(n) for n in ("dchain", "cnt_ok", "deg_ok", "sdeg_ok", "var_ok", "sdx_ok", "scale_ok"))
        bcast, be_ok, be_row, meta = (sem(n) for n in ("bcast", "be_ok", "be_row", "meta"))
        t_made, split0, t1_stored = (sem(n) for n in ("t_made", "split0", "t1_stored"))
        wl_ld, w_tr, w_cp, beta_made, bias_mm, w_done = (
            sem(n) for n in ("wl_ld", "w_tr", "w_cp", "beta_made", "bias_mm", "w_done"))
        got = [[sem(f"got{l}_{j}") for j in range(RING)] for l in range(2)]

        def two(name):
            return [sem(f"{name}{l}") for l in range(2)]
        idx_set, idx_read = two("idx_set"), two("idx_read")
        arrived, freed, s_free, s_ready, s_abs, s_iota = (
            two(n) for n in ("arrived", "freed", "s_free", "s_ready", "s_abs", "s_iota"))
        agg_done, agg_out, agg_tr, aggT_ok, mm_done, mm_read, tin_ld, tin_used, res_ok = (
            two(n) for n in ("agg_done", "agg_out", "agg_tr", "aggT_ok", "mm_done", "mm_read", "tin_ld", "tin_used", "res_ok"))
        v1_ok, sd1_ok, v2_ok, sd2_ok, z_ok, z_tr, zT_ok, split_ok, t2_stored, zT_stored = (
            sem(n) for n in ("v1_ok", "sd1_ok", "v2_ok", "sd2_ok", "z_ok", "z_tr", "zT_ok", "split_ok", "t2_stored", "zT_stored"))
        out_stored = sem("out_stored")
        passed, passed_v = sem("passed"), sem("passed_v")
        vchain = sem("vchain")

        block = ctx.enter_context(nc.Block())

        @block.sync
        def _(sp):
            sp.dma_start(d125[0:HP, :], dst.rearrange("(p c) -> p c", p=HP)).then_inc(ld_d125, 16)
            sp.wait_ge(natz, 2)
            whole = (BC - 1) * P
            for nat, e in ((natd, dst), (nats, src)):
                sp.dma_start(nat[:, 0:whole].rearrange("p (c l) -> p c l", l=P),
                             e[0:whole * P].rearrange("(c p l) -> p c l", p=P, l=P)).then_inc(ld_nat, 16)
                sp.dma_start(nat[0:FULLB - whole, whole:whole + P],
                             e[whole * P:FULLB * P].rearrange("(p l) -> p l", l=P)).then_inc(ld_nat, 16)
                sp.dma_start(nat[FULLB - whole:NB - whole, whole:whole + E - FULLB * P],
                             e[FULLB * P:E].rearrange("(p l) -> p l", p=1)).then_inc(ld_nat, 16)
            sp.dma_start(b0_sb[:, :], b0.rearrange("(a d) -> a d", a=1).broadcast_to((P, D))).then_inc(ld_small, 16)
            sp.dma_start(Br[:, :], b_l.rearrange("(a d) -> a d", a=1).broadcast_to((P, D))).then_inc(ld_small, 16)
            with nc.allow_non_contiguous_dma("512 numbers, once"):
                sp.dma_start(gcol[:, :], gamma.rearrange("(c p) -> p c", p=P)).then_inc(ld_small, 16)
                sp.dma_start(bcol[:, :], beta.rearrange("(c p) -> p c", p=P)).then_inc(ld_small, 16)
            for g in range(XG):
                t0 = g * X_GROUP
                n = X_GROUP if g < XG - 1 else X_GROUP - 1
                sp.dma_start(nodes[:, t0 * D:(t0 + n) * D].rearrange("p (t d) -> p t d", d=D),
                             x[t0 * P:(t0 + n) * P, :].rearrange("(t p) d -> p t d", p=P)).then_inc(ld_x[g], 16)
                if g == XG - 1:
                    sp.wait_ge(consts, 1)
                    sp.dma_start(nodes[0:LAST, (NT - 1) * D:NT * D], x[(NT - 1) * P:N, :]).then_inc(ld_x[g], 16)
            sp.wait_ge(hist, 1)
            sp.dma_start(w0_sb[:, :].rearrange("p (c n) -> p c n", n=D),
                         W0.rearrange("(c p) n -> p c n", p=P)).then_inc(ld_w, 16)
            for n, w in enumerate((w_l, w_r)):
                if n == 1:
                    sp.wait_ge(w_tr, KC)
                sp.dma_start(wnat.rearrange("p (c n) -> p c n", n=D),
                             w.rearrange("(c p) n -> p c n", p=P)).then_inc(wl_ld, 16)
            for g in range(XG):
                sp.wait_ge(split0, X_GROUP * (g + 1))
                t0 = g * X_GROUP
                sp.dma_start(table[0][t0 * P:(t0 + X_GROUP) * P, :].rearrange("(t p) c -> p t c", p=P),
                             nodes16[:, t0 * 2 * D:(t0 + X_GROUP) * 2 * D].rearrange("p (t c) -> p t c", c=2 * D)
                             ).then_inc(t1_stored, 16)
            for l in range(2):
                with sp.Fori(0, GROUPS) as g:
                    for j in range(RING):
                        sp.wait_ge(got[l][j], g * 16 + 16)
                        if j % QUAD == QUAD - 1:
                            sp.sem_inc(arrived[l], 1)

        @block.gpsimd
        def _(pool):
            pool.memset(natd, -1).then_inc(natz, 1)
            pool.memset(nats, 0).then_inc(natz, 1)
            pool.iota(iotax[:, 0:NT * HIST_COLS], [[1, NT], [0, HIST_COLS]], base=0, channel_multiplier=0,
                      allow_small_or_imprecise_dtypes=True).then_inc(digits, 1)
            pool.iota(iotax[:, NT * HIST_COLS:], [[1, P], [0, HIST_COLS]], base=0, channel_multiplier=0,
                      allow_small_or_imprecise_dtypes=True).then_inc(digits, 1)
            pool.memset(nodes[:, (NT - 1) * D:NT * D], 0.0).then_inc(consts, 1)
            for t, v in ((ident, 0.0), (ident16, 0.0), (zero16, 0.0), (onesf, 1.0), (last_lane, 1.0), (eps, EPS), (one_c, 1.0)):
                pool.memset(t[:, :], v).then_inc(consts, 1)
            pool.iota(iotaf[:, :], [[1, P]], base=0, channel_multiplier=0,
                      allow_small_or_imprecise_dtypes=True).then_inc(consts, 1)
            pool.iota(tile0[:, :], [[P, NT]], base=0, channel_multiplier=0,
                      allow_small_or_imprecise_dtypes=True).then_inc(consts, 1)
            pool.iota(thr[:, :], [[0, 1]], base=P, channel_multiplier=P,
                      allow_small_or_imprecise_dtypes=True).then_inc(consts, 1)
            pool.wait_ge(consts, 11)
            for m in (ident, ident16):
                pool.affine_select(out=m[:, :], in_=m[:, :], compare_op=ALU.not_equal, fill=1.0,
                                   base=0, pattern=[[-1, P]], channel_multiplier=1).then_inc(consts, 1)
            pool.affine_select(out=last_lane[:, :], in_=last_lane[:, :], compare_op=ALU.is_ge, fill=0.0,
                               base=-(P - 1), pattern=[[0, P]], channel_multiplier=1).then_inc(consts, 1)
            for l in range(2):
                if l == 0:
                    pool.wait_ge(t1_stored, 16 * XG)
                    pool.wait_ge(meta, 2)
                else:
                    pool.wait_ge(t2_stored, 16 * NT)
                    pool.wait_ge(arrived[0], NQ)
                    pool.wait_ge(s_free[0], STEPS + SQ)
                pool.sem_inc(freed[l], RQ)

                def gather_round(g, q):
                    for j in range(RING):
                        if j % QUAD == 0:
                            pool.wait_ge(freed[l], g * RQ + (j // QUAD + 1))
                            pool.sem_inc(passed, 1)
                        if j == 0:
                            pool.tensor_copy(idx[:, q * RING:(q + 1) * RING], srcT[:, ds(g * RING, RING)]).then_inc(idx_set[l], 1)
                            pool.wait_ge(idx_set[l], g + 1)
                            pool.sem_inc(passed, 1)
                        c = q * RING + j
                        pool.indirect_dma_start(
                            out=ring[:, j * 2 * D:(j + 1) * 2 * D], out_offset=None, in_=table[l],
                            in_offset=bass.IndirectOffsetOnAxis(ap=idx[:, c:c + 1], axis=0)).then_inc(got[l][j], 16)

                assert GROUPS % 2 == 1
                with pool.Fori(0, GROUPS - 1, 2) as g:
                    gather_round(g, 0)
                    gather_round(g + 1, 1)
                gather_round(GROUPS - 1, 0)

        def live(T, back, count=NT):
            return not isinstance(T, int) or 0 <= T - back < count

        def tiles(eng, body, drain):
            for T in range(4):
                body(T, T % 2)
            assert NT % 2 == 1
            with eng.Fori(4, NT - 1, 2) as T:
                body(T, 0)
                body(T + 1, 1)
            for T in range(NT - 1, NT + drain):
                body(T, T % 2)

        @block.scalar
        def _(act):
            act.wait_ge(consts, 14)
            for n, w in enumerate((wl_sb, wr_sb)):
                for c in range(KC):
                    act.wait_ge(w_tr, n * KC + c + 1)
                    if n == 0 and c == 0:
                        act.wait_ge(nat_tr, 2 * BC)
                    nc.scalar.activation(w[:, c * D:(c + 1) * D], ztp[:, :], ACT.Copy).then_inc(w_cp, 1)
            act.wait_ge(deg_ok, 1)
            nc.scalar.activation(sdeg, deg, ACT.Sqrt).then_inc(sdeg_ok, 1)
            act.wait_ge(var_ok, NT)
            nc.scalar.activation(sdx, mv0[:, :, 1], ACT.Sqrt, bias=eps[:, :]).then_inc(sdx_ok, 1)
            act.wait_ge(scale_ok, 1)
            def scaled(T, q):
                nc.scalar.activation(t32[:, q * D:(q + 1) * D], nodes[:, ds(T * D, D)], ACT.Relu,
                                     bias=bias0[:, ds(T, 1)], scale=scale0[:, ds(T, 1)]).then_inc(t_made, 1)

            scaled(0, 0)
            scaled(1, 1)
            with act.Fori(2, NT - 1, 2) as T:
                for q in range(2):
                    act.wait_ge(split0, T + q - 1)
                    scaled(T + q, q)
            act.wait_ge(split0, NT - 2)
            scaled(NT - 1, 0)

            def selection(l, T):
                lo = act.value_load(be_i[0:1, ds(T, 1)], min_val=0, max_val=NQ - 1)
                hi = act.value_load(be_i[0:1, ds(T + 1, 1)], min_val=0, max_val=NQ - 1)
                nc.scalar.activation(iota_t[:, :], iotaf[:, :], ACT.Identity, bias=tile0[:, ds(T, 1)]).then_inc(s_iota[l], 1)
                act.wait_ge(s_iota[l], T + 1)
                with act.Fori(lo, hi + 1) as qd:
                    act.wait_ge(s_free[l], qd + T + 1)
                    o = ((qd + T) & 1) * (QUAD * P)
                    for j in range(QUAD):
                        ins = nc.scalar.activation(absd[:, ds(o + j * P, P)], iota_t[:, :], ACT.Abs,
                                                   bias=dstT[:, ds(qd * QUAD + j, 1)], scale=-1.0)
                    ins.then_inc(s_abs[l], 1)
                    act.wait_ge(s_abs[l], qd + T + 1)
                    nc.scalar.activation(sel[:, ds(((qd + T) & (SQ - 1)) * (QUAD * P), QUAD * P)],
                                         absd[:, ds(o, QUAD * P)], ACT.Relu,
                                         bias=one_c[:, :], scale=-1.0).then_inc(s_ready[l], 1)

            def load_x(T, q):
                if live(T, 2):
                    act.wait_ge(tin_used[0], T - 1)
                if live(T, 1):
                    act.wait_ge(tin_ld[0], T * 16)
                rows = LAST if isinstance(T, int) and T == NT - 1 else P
                act.dma_start(xin[0:rows, q * D:(q + 1) * D], x[ds(T * P, rows), :]).then_inc(tin_ld[0], 16)

            def store_table(T, q):
                act.wait_ge(split_ok, T + 1)
                if live(T, 1):
                    act.wait_ge(t2_stored, T * 16)
                act.dma_start(table[1][ds(T * P, P), :], stage[:, q * 2 * D:(q + 1) * 2 * D]).then_inc(t2_stored, 16)

            def store_zT(T):
                act.wait_ge(zT_ok, T + 1)
                if live(T, 1):
                    act.wait_ge(zT_stored, T * 16)
                act.dma_start(xT_dram[ds(T * P, P), :], zT).then_inc(zT_stored, 16)

            def first_phase(T, q):
                if live(T, 0):
                    selection(0, T)
                if live(T, 1):
                    load_x(T - 1, 1 - q)
                if live(T, 3):
                    store_table(T - 3, 1 - q)
                if live(T, 4):
                    store_zT(T - 4)

            act.wait_ge(be_row, 2)
            act.wait_ge(split0, NT)
            act.sem_inc(s_free[0], SQ)
            tiles(act, first_phase, 4)
            act.wait_ge(zT_stored, 16 * NT)

            def load_xT(T, q):
                if live(T, 2):
                    act.wait_ge(mm_done[1], T - 1)
                if live(T, 1):
                    act.wait_ge(tin_ld[1], T * 16)
                act.dma_start(xin[:, q * D:(q + 1) * D], xT_dram[ds(T * P, P), :]).then_inc(tin_ld[1], 16)

            def store_out(T, q):
                act.wait_ge(res_ok[1], T + 1)
                if live(T, 1):
                    act.wait_ge(out_stored, T * 16)
                rows = LAST if isinstance(T, int) and T == NT - 1 else P
                act.dma_start(out[ds(T * P, rows), :], res[0:rows, q * D:(q + 1) * D]).then_inc(out_stored, 16)

            def second_phase(T, q):
                if live(T, 0):
                    selection(1, T)
                if live(T, 1):
                    load_xT(T - 1, 1 - q)
                if live(T, 3):
                    store_out(T - 3, 1 - q)

            act.wait_ge(s_free[0], STEPS + SQ)
            act.wait_ge(tin_used[0], NT)
            act.sem_inc(s_free[1], SQ)
            tiles(act, second_phase, 3)
            act.wait_ge(out_stored, 16 * NT)

        @block.tensor
        def _(pe):
            pe.wait_ge(consts, 14)
            pe.wait_ge(nat_cast, 2)
            for k in range(2 * BC):
                bk = (misc, misc2)[k % 2]
                if k >= 2:
                    pe.wait_ge(nat_cp, k - 1)
                pe.transpose(bk[:, 0:P], natf[:, k * P:(k + 1) * P], ident[:, :]).then_inc(nat_tr, 1)
            pe.wait_ge(nat_cp, 2 * BC)
            ends = dstT[:, 0:NQ * QUAD].rearrange("p (q j) -> p q j", j=QUAD)[:, 0:NQ - 1, QUAD - 1]
            pe.matmul(outp[:, 0:NQ - 1], last_lane[:, :], ends, start=True, stop=True).then_inc(bcast, 1)
            pe.wait_ge(meta, 1)
            for k in range(CHUNKS):
                pe.wait_ge(oh_made, k + 1)
                o = (k % 2) * OH
                v = onehot[0:HP, o:o + OH].rearrange("p (v c) -> p v c", c=HIST_COLS)
                for c in range(HIST_COLS):
                    mm = pe.matmul(misc[0:NT, 0:P], v[:, 0:NT, c], v[:, NT:DIG, c],
                                   start=(k == 0 and c == 0), stop=(k == CHUNKS - 1 and c == HIST_COLS - 1))
                mm.then_inc(oh_used, 1)
            pe.wait_ge(hist, 1)
            pe.transpose(misc2[:, 0:NT], hcnt, ident[0:NT, 0:NT]).then_inc(cnt_ok, 1)
            pe.wait_ge(be_ok, 1)
            pe.matmul(misc[0:1, 0:NT], be_c[0:NT, :], ident[0:NT, 0:NT], start=True, stop=True,
                      skip_group_check=True).then_inc(be_row, 1)
            for n in range(2):
                pe.wait_ge(wl_ld, 16 * (n + 1))
                for c in range(KC):
                    if n or c:
                        pe.wait_ge(w_cp, n * KC + c)
                    for r in range(KC):
                        mm = pe.transpose(ztp[:, r * P:(r + 1) * P], wnat[:, r * D + c * P:r * D + (c + 1) * P], ident[:, :])
                    mm.then_inc(w_tr, 1)
            pe.wait_ge(beta_made, KC)
            pe.wait_ge(w_cp, 2 * KC)
            for w, bk in ((wl_sb, outp), (wr_sb, trp)):
                for c in range(KC):
                    mm = pe.matmul(bk[:, :], beta_b[:, c * P:(c + 1) * P], w[:, c * D:(c + 1) * D],
                                   start=(c == 0), stop=(c == KC - 1))
                mm.then_inc(bias_mm, 1)
            pe.wait_ge(ld_w, 16)
            pe.wait_ge(split0, NT)

            def gathered(l, T, q):
                a = aggp[:, q * 512:(q + 1) * 512]
                lo = pe.value_load(be_i[0:1, ds(T, 1)], min_val=0, max_val=NQ - 1)
                hi = pe.value_load(be_i[0:1, ds(T + 1, 1)], min_val=0, max_val=NQ - 1)
                if live(T, 2):
                    pe.wait_ge(agg_out[l], T - 1)

                def quad(qd, first):
                    pe.wait_ge(arrived[l], qd + 1)
                    pe.wait_ge(s_ready[l], qd + T + 1)
                    o = ((qd + T) & (SQ - 1)) * (QUAD * P)
                    r = (qd & (RQ - 1)) * (QUAD * 2 * D)
                    for j in range(QUAD):
                        s = sel[:, ds(o + j * P, P)]
                        mm = pe.matmul(a, s, ring[:, ds(r + j * 2 * D, D)], start=first and j == 0, stop=False,
                                       skip_group_check=True)
                        if not first and j == 0:
                            mm.then_inc(freed[l], 1)
                        mm = pe.matmul(a, s, ring[:, ds(r + j * 2 * D + D, D)], start=False, stop=False,
                                       skip_group_check=True)
                    mm.then_inc(s_free[l], 1)

                quad(lo, True)
                with pe.If(lo < hi):
                    with pe.Fori(lo + 1, hi + 1) as qd:
                        quad(qd, False)
                if l == 0:
                    pe.matmul(a, ident16[:, :], nodes16[:, ds(T * 2 * D, D)], start=False, stop=False, skip_group_check=True)
                    mm = pe.matmul(a, ident16[:, :], nodes16[:, ds(T * 2 * D + D, D)], start=False, stop=True,
                                   skip_group_check=True)
                else:
                    mm = pe.matmul(a, ident16[:, :], zero16[:, :], start=False, stop=True, skip_group_check=True)
                mm.then_inc(agg_done[l], 1)

            def turn_agg(l, T, q):
                pe.wait_ge(agg_out[l], T + 1)
                if live(T, 1):
                    pe.wait_ge(aggT_ok[l], T)
                for c in range(KC):
                    mm = pe.transpose(trp[:, c * P:(c + 1) * P], agg[:, q * D + c * P:q * D + (c + 1) * P], ident[:, :])
                mm.then_inc(agg_tr[l], 1)

            def project(l, T, q, w, more=None):
                pe.wait_ge(aggT_ok[l], T + 1)
                if live(T, 1):
                    pe.wait_ge(mm_read[l], T)
                for c in range(KC):
                    mm = pe.matmul(outp[:, :], aggT[:, c * P:(c + 1) * P], w[:, c * D:(c + 1) * D],
                                   start=(c == 0), stop=(c == KC - 1 and more is None))
                if more is not None:
                    pe.wait_ge(tin_ld[l], T * 16 + 16)
                    for c in range(KC):
                        mm = pe.matmul(outp[:, :], xin[:, q * D + c * P:q * D + (c + 1) * P], more[:, c * D:(c + 1) * D],
                                       start=False, stop=(c == KC - 1))
                mm.then_inc(mm_done[l], 1)

            def turn_z(T):
                pe.wait_ge(split_ok, T + 1)
                if live(T, 1):
                    pe.wait_ge(zT_ok, T)
                for c in range(KC):
                    mm = pe.transpose(ztp[:, c * P:(c + 1) * P], zs[:, c * P:(c + 1) * P], ident[:, :])
                mm.then_inc(z_tr, 1)

            def first_phase(T, q):
                if live(T, 0):
                    gathered(0, T, q)
                if live(T, 2):
                    project(0, T - 2, q, w0_sb)
                if live(T, 3):
                    turn_z(T - 3)
                if live(T, 1):
                    turn_agg(0, T - 1, 1 - q)

            def second_phase(T, q):
                if live(T, 0):
                    gathered(1, T, q)
                if live(T, 2):
                    project(1, T - 2, q, wl_sb, wr_sb)
                if live(T, 1):
                    turn_agg(1, T - 1, 1 - q)

            tiles(pe, first_phase, 3)
            pe.wait_ge(agg_out[0], NT)
            pe.wait_ge(w_done, 2 * KC)
            tiles(pe, second_phase, 2)

        @block.vector
        def _(dve):
            v = nc.vector
            link_n = [0]

            def link(ins, sem_=dchain):
                link_n[0] += 1
                ins.then_inc(dchain, 1)
                dve.wait_ge(dchain, link_n[0])

            dve.wait_ge(ld_nat, 96)
            v.tensor_copy(natf[:, 0:BC * P], natd).then_inc(nat_cast, 1)
            v.tensor_copy(natf[:, BC * P:2 * BC * P], nats).then_inc(nat_cast, 1)
            for k in range(2 * BC):
                bk = (misc, misc2)[k % 2]
                dve.wait_ge(nat_tr, k + 1)
                to = dstT if k < BC else srcT
                b = (k % BC) * P
                n = min(P, NQ * QUAD - b)
                v.tensor_copy(to[:, b:b + n], bk[:, 0:n]).then_inc(nat_cp, 1)
            dve.wait_ge(nat_cp, 2 * BC)
            v.memset(be_i[0:1, 0:1], 0).then_inc(meta, 1)
            v.memset(be_c[:, :], 0.0).then_inc(meta, 1)
            dve.wait_ge(ld_d125, 16)
            v.tensor_scalar(dig_i[0:HP, 0:HC], d125[0:HP, :], 7, None, ALU.arith_shift_right).then_inc(digits, 1)
            v.tensor_scalar(dig_i[0:HP, HC:2 * HC], d125[0:HP, :], P - 1, None, ALU.bitwise_and).then_inc(digits, 1)
            dve.wait_ge(digits, 4)
            v.tensor_copy(dig[0:HP, :], dig_i[0:HP, :]).then_inc(digits, 1)
            dve.wait_ge(digits, 5)
            for k in range(CHUNKS):
                if k >= 2:
                    dve.wait_ge(oh_used, k - 1)
                o = (k % 2) * OH
                for a, n, d0 in ((0, NT, 0), (NT, P, HC)):
                    ins = v.tensor_tensor(
                        onehot[0:HP, o + a * HIST_COLS:o + (a + n) * HIST_COLS].rearrange("p (v c) -> p v c", c=HIST_COLS),
                        dig[0:HP, d0 + k * HIST_COLS:d0 + (k + 1) * HIST_COLS].rearrange("p (a c) -> p a c", a=1).broadcast_to((HP, n, HIST_COLS)),
                        iotax[0:HP, a * HIST_COLS:(a + n) * HIST_COLS].rearrange("p (v c) -> p v c", c=HIST_COLS),
                        ALU.is_equal)
                ins.then_inc(oh_made, 1)
            dve.wait_ge(oh_used, CHUNKS)
            v.tensor_copy(hcnt, misc[0:NT, 0:P]).then_inc(hist, 1)
            dve.wait_ge(bcast, 1)
            v.tensor_scalar(act_sum[:, 0:NQ - 1], outp[:, 0:NQ - 1], thr[:, :], 0.0, ALU.is_lt, ALU.add,
                            accum_out=be_c[:, 0:1]).then_inc(be_ok, 1)
            dve.wait_ge(be_ok, 1)
            dve.wait_ge(cnt_ok, 1)
            link(v.tensor_copy(cnt[:, :], misc2[:, 0:NT]))
            v.tensor_scalar(deg, cnt[:, :], 1.0, None, ALU.add).then_inc(deg_ok, 1)
            dve.wait_ge(be_row, 1)
            v.tensor_copy(be_i[0:1, 1:NT + 1], misc[0:1, 0:NT]).then_inc(be_row, 1)
            link(v.tensor_scalar(has, cnt[:, :], 1.0, None, ALU.min))
            link(v.tensor_scalar(cinv_up, cnt[:, :], 1.0, None, ALU.max))
            link(v.reciprocal(cinv_up, cinv_up))
            link(v.tensor_scalar(cinv_up, cinv_up, 1.0 / UP, None, ALU.mult))
            dve.wait_ge(ld_small, 64)
            for c in range(KC):
                v.tensor_scalar(beta_b[:, c * P:(c + 1) * P], onesf[:, :], bcol[:, c:c + 1], None,
                                ALU.mult).then_inc(beta_made, 1)
            for T in range(NT):
                if T % X_GROUP == 0:
                    g = T // X_GROUP
                    dve.wait_ge(ld_x[g], 32 if g == XG - 1 else 16)
                link(v.bn_stats(stats0[:, T, :], nodes[:, T * D:(T + 1) * D]))
                v.bn_aggr(mv0[:, T, :], stats0[:, T, :]).then_inc(var_ok, 1)
            dve.wait_ge(sdeg_ok, 1)
            link(v.reciprocal(dinv, sdeg))
            link(v.tensor_scalar(dinv_up, dinv, 1.0 / UP, None, ALU.mult))
            dve.wait_ge(sdx_ok, 1)
            link(v.reciprocal(rstd0, sdx))
            link(v.tensor_tensor(scale0, rstd0, dinv, ALU.mult))
            link(v.tensor_scalar(scale0, scale0, UP, None, ALU.mult))
            v.scalar_tensor_tensor(bias0, mv0[:, :, 0], -1.0, scale0, ALU.mult, ALU.mult).then_inc(scale_ok, 1)
            with dve.Fori(0, NT) as T:
                dve.wait_ge(t_made, T + 1)
                t = t32[:, ds((T % 2) * D, D)]
                v.tensor_copy(nodes16[:, ds(T * 2 * D, D)], t).then_inc(vchain, 1)
                dve.wait_ge(vchain, T + 1)
                v.tensor_tensor(nodes16[:, ds(T * 2 * D + D, D)], t, nodes16[:, ds(T * 2 * D, D)],
                                ALU.subtract).then_inc(split0, 1)
            dve.wait_ge(bias_mm, 2)
            link(v.tensor_copy(Bl[:, :], outp[:, :]))
            link(v.tensor_tensor(Br[:, :], trp[:, :], Br[:, :], ALU.add))
            for w, up in ((wl_sb, 1.0), (wr_sb, 1.0 / UP)):
                for c in range(KC):
                    v.tensor_scalar(w[:, c * D:(c + 1) * D], w[:, c * D:(c + 1) * D], gcol[:, c:c + 1], up,
                                    ALU.mult, ALU.mult).then_inc(w_done, 1)

            def evacuate(l, T, q, by):
                dve.wait_ge(agg_done[l], T + 1)
                if live(T, 2):
                    dve.wait_ge(agg_tr[l], T - 1)
                v.tensor_scalar(agg[:, q * D:(q + 1) * D], aggp[:, q * 512:(q + 1) * 512], by[:, ds(T, 1)], None,
                                ALU.mult).then_inc(agg_out[l], 1)

            def copy_aggT(l, T):
                dve.wait_ge(agg_tr[l], T + 1)
                if live(T, 1):
                    dve.wait_ge(mm_done[l], T)
                v.tensor_copy(aggT, trp[:, :]).then_inc(aggT_ok[l], 1)

            def copy_zT(T):
                dve.wait_ge(z_tr, T + 1)
                if live(T, 1):
                    dve.wait_ge(zT_stored, T * 16)
                v.tensor_copy(zT, ztp[:, :]).then_inc(zT_ok, 1)

            y, v2, t2, u2 = (rs[:, 2 * n:2 * n + 2] for n in range(4))
            NEWTON = 3

            def norms(T, q):
                n = [0]

                def then(ins):
                    n[0] += 1
                    ins.then_inc(v0, 1)
                    dve.wait_ge(v0, T * LINKS + n[0])

                dve.wait_ge(mm_done[0], T + 1)
                v.tensor_tensor(act_sum, outp[:, :], b0_sb[:, :], ALU.add).then_inc(mm_read[0], 1)
                dve.wait_ge(mm_read[0], T + 1)
                dve.wait_ge(tin_ld[0], T * 16 + 16)
                v.scalar_tensor_tensor(x1, act_sum, 0.0, xin[:, q * D:(q + 1) * D], ALU.max, ALU.add).then_inc(tin_used[0], 1)
                dve.wait_ge(tin_used[0], T + 1)
                then(v.bn_stats(st[:, 0:6], x1))
                dve.sem_inc(passed_v, 1)
                then(v.bn_aggr(mv[:, 0:2], st[:, 0:6]))
                then(v.tensor_scalar(g1, x1, mv[:, 0:1], mv[:, 0:1], ALU.max, ALU.subtract))
                then(v.bn_stats(st[:, 6:12], g1))
                dve.sem_inc(passed_v, 1)
                then(v.bn_aggr(mv[:, 2:4], st[:, 6:12]))
                then(v.tensor_scalar(v2[:, 0:1], mv[:, 1:2], EPS, None, ALU.add))
                then(v.scalar_tensor_tensor(v2[:, 1:2], v2[:, 0:1], EPS, mv[:, 3:4], ALU.mult, ALU.add))
                then(v.tensor_scalar(t2.bitcast(I32), v2.bitcast(I32), 1, None, ALU.arith_shift_right))
                then(v.tensor_scalar(y.bitcast(I32), t2.bitcast(I32), -1.0, float(0x5F3759DF), ALU.mult, ALU.add))
                for _ in range(NEWTON):
                    then(v.tensor_tensor(t2, y, y, ALU.mult))
                    then(v.tensor_tensor(u2, t2, v2, ALU.mult))
                    then(v.tensor_scalar(t2, u2, -0.5, 1.5, ALU.mult, ALU.add))
                    then(v.tensor_tensor(y, y, t2, ALU.mult))
                then(v.tensor_scalar(u2[:, 1:2], y[:, 1:2], UP, None, ALU.mult))
                v.tensor_scalar(zs, g1, mv[:, 2:3], u2[:, 1:2], ALU.subtract, ALU.mult).then_inc(v0, 1)
                n[0] += 1
                v.scalar_tensor_tensor(nodes[:, ds(T * D, D)], g1, y[:, 0:1], x1, ALU.mult, ALU.add).then_inc(res_ok[0], 1)
                if live(T, 2):
                    dve.wait_ge(t2_stored, (T - 1) * 16)
                dve.wait_ge(v0, T * LINKS + n[0])
                s = q * 2 * D
                then(v.tensor_copy(stage[:, s:s + D], zs))
                v.tensor_tensor(stage[:, s + D:s + 2 * D], zs, stage[:, s:s + D], ALU.subtract).then_inc(split_ok, 1)
                dve.wait_ge(split_ok, T + 1)
                assert n[0] == LINKS

            LINKS = 11 + 4 * NEWTON + 1
            v0 = sem("v0")

            def first_phase(T, q):
                if live(T, 0):
                    evacuate(0, T, q, dinv_up)
                if live(T, 1):
                    copy_aggT(0, T - 1)
                if live(T, 3):
                    copy_zT(T - 3)
                if live(T, 2):
                    norms(T - 2, q)

            def result(T, q):
                dve.wait_ge(mm_done[1], T + 1)
                v.scalar_tensor_tensor(act_sum, Bl[:, :], has[:, ds(T, 1)], outp[:, :], ALU.mult, ALU.add).then_inc(mm_read[1], 1)
                dve.wait_ge(mm_read[1], T + 1)
                v.tensor_tensor(x1, act_sum, Br[:, :], ALU.add).then_inc(tin_used[1], 1)
                dve.wait_ge(tin_used[1], T + 1)
                if live(T, 2):
                    dve.wait_ge(out_stored, (T - 1) * 16)
                else:
                    dve.wait_ge(t2_stored, NT * 16)
                v.scalar_tensor_tensor(res[:, q * D:(q + 1) * D], x1, 0.0, nodes[:, ds(T * D, D)], ALU.max,
                                       ALU.add).then_inc(res_ok[1], 1)

            def second_phase(T, q):
                if live(T, 0):
                    evacuate(1, T, q, cinv_up)
                if live(T, 1):
                    copy_aggT(1, T - 1)
                if live(T, 2):
                    result(T - 2, q)

            tiles(dve, first_phase, 3)
            tiles(dve, second_phase, 2)


_INS = ['x', 'src', 'dst', 'L0_gnn_W', 'L0_gnn_b', 'L1_gnn_ln_gamma', 'L1_gnn_ln_beta', 'L1_gnn_w_l', 'L1_gnn_b_l', 'L1_gnn_w_r']


def kernel(**inputs):
    import numpy as _np
    import concourse.bacc as _bacc
    from concourse import mybir as _mybir
    from concourse.bass_utils import run_bass_kernel_spmd as _run

    nc = _bacc.Bacc("TRN2", target_bir_lowering=False, num_devices=1)
    arrays, args = {}, []
    for name in _INS:
        a = _np.ascontiguousarray(inputs[name])
        arrays[f"in_{name}_dram"] = a
        args.append(nc.dram_tensor(f"in_{name}_dram", a.shape, _mybir.dt.from_np(a.dtype), kind="ExternalInput").ap())
    shape = inputs['x'].shape
    out = nc.dram_tensor("out_0_dram", shape, _mybir.dt.float32, kind="ExternalOutput").ap()
    gnn_kernel(nc, *args, out)
    r = _run(nc, [arrays], core_ids=[0])
    return r.results[0]["out_0_dram"]
```

```python
from contextlib import ExitStack

import concourse.bass as bass
from concourse import mybir

ALU = mybir.AluOpType
ACT = mybir.ActivationFunctionType
F32 = mybir.dt.float32
F16 = mybir.dt.float16
I32 = mybir.dt.int32
U32 = mybir.dt.uint32

P = 128
QUAD_BITS = 2
QUAD = 1 << QUAD_BITS
RING = 16
RQ = RING // QUAD
NEWTON = 3
SQ = 8
EPS = 1e-5
UP = 2048.0
HIST_COLS = 40
X_GROUP = 7


def ds(start, size):
    return bass.ds(start, size)


def gnn_kernel(nc, x, src, dst, W0, b0, gamma, beta, w_l, b_l, w_r, out):
    N, D = x.shape
    E = src.shape[0]
    KC = D // P
    NT = (N + P - 1) // P
    LAST = N - (NT - 1) * P
    NB = (E + P - 1) // P
    FULLB = E // P
    BC = (NB + P - 1) // P
    NQ = (NB + QUAD - 1) // QUAD
    STEPS = NQ + NT - 1
    GROUPS = (NB + RING - 1) // RING
    HP = 125
    HC = E // HP
    CHUNKS = HC // HIST_COLS
    XG = NT // X_GROUP
    T1_CUTS = [*range(0, NT - 5, 6), NT - 2, NT]
    ENDS = (0, min(512, NB - 1), NB - 1)
    TURNS = (((NT + 1, 2), (NT + 2, 2), (NT + 3, 2), (NT + 4, 3)), ((0, 2), (1, 2)))
    BETWEEN = sum(n for _, n in TURNS[0])
    OWN = BETWEEN + sum(n for _, n in TURNS[1])
    EARLY = NT - OWN
    DIG = NT + P
    assert 4 < BC <= 8
    assert HP * HC == E and CHUNKS * HIST_COLS == HC and XG * X_GROUP == NT and D == 512

    table = [nc.dram_tensor(f"table{n}", [NT * P, 2 * D], F16, kind="Internal").ap() for n in range(2)]
    xT_dram = nc.dram_tensor("xT_dram", [NT * P, D], F32, kind="Internal").ap()

    with ExitStack() as ctx:
        def sb(name, shape, dt):
            return ctx.enter_context(nc.sbuf_tensor(name, shape, dt))

        def bank(name):
            return ctx.enter_context(nc.psum_tensor(name, [P, 512], F32))

        def sem(name):
            return ctx.enter_context(nc.semaphore(name))

        nodes = sb("nodes", [P, NT * D], F32)
        nodes16 = nodes[:, :].bitcast(F16)
        ring = sb("ring", [P, RING * 2 * D], F16)
        sel = sb("sel", [P, SQ * QUAD * P], F16)
        weights = sb("weights", [P, 3 * KC * D], F32)
        w0_sb, wl_sb, wr_sb = (weights[:, n * KC * D:(n + 1) * KC * D] for n in range(3))
        b0_sb = sb("b0_sb", [P, D], F32)
        Bl = sb("Bl", [P, D], F32)
        Br = sb("Br", [P, D], F32)
        work = sb("work", [P, 13 * D], F32)

        def wk(n):
            return work[:, n * D:(n + 1) * D]
        agg = work[:, 0:2 * D]
        aggT, act_sum, x1, zs = wk(2), wk(3), wk(4), wk(6)
        g1 = work[:, 4 * D:6 * D]
        zT = work[:, 7 * D:9 * D]
        beta_b = act_sum
        stage = work[:, 9 * D:11 * D].bitcast(F16)
        res = work[:, 9 * D:11 * D]
        xin = work[:, 11 * D:13 * D]
        dstT = sb("dstT", [P, NQ * QUAD], F32)
        srcT = sb("srcT", [P, NQ * QUAD], U32)
        idx = sb("idx", [P, 2 * RING], U32)
        iotaf = sb("iotaf", [P, P], F32)
        tile0 = sb("tile0", [P, NT], F32)
        thr = sb("thr", [P, 1], F32)
        ident = sb("ident", [P, P], F32)
        ident16 = sb("ident16", [P, P], F16)
        zero16 = sb("zero16", [P, 2], F16)
        iota_t = sb("iota_t", [P, P], F32)
        absd = sb("absd", [P, 2 * QUAD * P], F16)
        eps = sb("eps", [P, 1], F32)
        one_c = sb("one_c", [P, 1], F32)
        gcol = sb("gcol", [P, KC], F32)
        bcol = sb("bcol", [P, KC], F32)
        cnt = sb("cnt", [P, NT], F32)
        cols = sb("cols", [P, 12, NT], F32)
        deg, sdeg, dinv, sdx, rstd0, scale0, bias0, dinv_up, cinv_up, has, sum0, ssq0 = (cols[:, n, :] for n in range(12))
        be_c = sb("be_c", [P, 2], F32)
        tile_block = sb("tile_block", [1, NT + 1], I32)
        tile_quad = sb("tile_quad", [1, NT + 1], I32)
        st = sb("st", [P, 12], F32)
        mv = sb("mv", [P, 8], F32)
        rs = sb("rs", [P, 8], F32)
        natd = sel[:, 0:2 * BC * P].bitcast(I32)
        nats = sel[:, 2 * BC * P:4 * BC * P].bitcast(I32)
        natf = weights[:, 0:2 * BC * P]
        dig_i = work[:, 0:2 * HC].bitcast(I32)
        dig = work[:, 2 * HC:3 * HC].bitcast(F16)
        iotax = weights[:, KC * D:KC * D + DIG * HIST_COLS // 2].bitcast(F16)
        onehot = ring[:, :]
        t32 = ring[:, :].bitcast(F32)
        OH = DIG * HIST_COLS
        d125 = ring[:, 2 * OH:2 * OH + 2 * HC].bitcast(I32)
        hcnt = sel[0:NT, 4 * BC * P:4 * BC * P + 2 * P].bitcast(F32)
        last_lane = sel[:, 4 * BC * P + 2 * P:4 * BC * P + 4 * P].bitcast(F32)
        wnat = work[:, 3 * HC:3 * HC + 8 * D]
        nmean0 = bias0

        aggp = ctx.enter_context(nc.psum_tensor("aggp", [P, 2 * 512], F32))
        trp, outp, ztp, misc, misc2 = (bank(n) for n in ("trp", "outp", "ztp", "misc", "misc2"))
        outs = (outp, misc)

        EDGE_BANKS = (trp, ztp, outp, misc2)

        def own_place(k):
            z = xin if k < BETWEEN else work[:, 5 * D:7 * D]
            return z[:, k % 2 * D:(k % 2 + 1) * D], (misc2, trp if k < BETWEEN else ztp)[k % 2]
        own_out = w0_sb[:, 0:2 * D]

        ld_d125, ld_nat, ld_w, ld_small = (sem(n) for n in ("ld_d125", "ld_nat", "ld_w", "ld_small"))
        ld_x = [sem(f"ld_x{g}") for g in range(XG)]
        consts, natz, nat_cast, nat_tr, nat_cp = (sem(n) for n in ("consts", "natz", "nat_cast", "nat_tr", "nat_cp"))
        digits, oh_made, oh_used, hist, iota_ok = (sem(n) for n in ("digits", "oh_made", "oh_used", "hist", "iota_ok"))
        dchain, cnt_ok, deg_ok, sdeg_ok, mean_ok, var_ok, sdx_ok, scale_ok = (
            sem(n) for n in ("dchain", "cnt_ok", "deg_ok", "sdeg_ok", "mean_ok", "var_ok", "sdx_ok", "scale_ok"))
        bcast, be_ok, be_row, meta = (sem(n) for n in ("bcast", "be_ok", "be_row", "meta"))
        t_made, hi_made, hip_made, split0, t1_stored = (sem(n) for n in ("t_made", "hi_made", "hip_made", "split0", "t1_stored"))
        wl_ld, w_tr, w_cp, beta_made, bias_mm, w_done = (
            sem(n) for n in ("wl_ld", "w_tr", "w_cp", "beta_made", "bias_mm", "w_done"))
        got = [[sem(f"got{l}_{j}") for j in range(RING)] for l in range(2)]

        def two(name):
            return [sem(f"{name}{l}") for l in range(2)]
        idx_set = two("idx_set")
        arrived, freed, s_free, s_ready, s_abs, s_iota = (
            two(n) for n in ("arrived", "freed", "s_free", "s_ready", "s_abs", "s_iota"))
        agg_done, agg_out, agg_tr, aggT_ok, mm_done, mm_read, tin_ld, tin_used, res_ok = (
            two(n) for n in ("agg_done", "agg_out", "agg_tr", "aggT_ok", "mm_done", "mm_read", "tin_ld", "tin_used", "res_ok"))
        z_tr, zT_ok, split_ok, t2_stored, zT_stored = (
            sem(n) for n in ("z_tr", "zT_ok", "split_ok", "t2_stored", "zT_stored"))
        out_stored = sem("out_stored")
        own_ld, own_mm, own_cp, own_stored, own_used = (
            sem(n) for n in ("own_ld", "own_mm", "own_cp", "own_stored", "own_used"))
        passed, passed_v = sem("passed"), sem("passed_v")
        va, vb = sem("va"), sem("vb")

        block = ctx.enter_context(nc.Block())

        def t32_of(q):
            return t32[:, q * D:(q + 1) * D]

        @block.sync
        def _(sp):
            sp.dma_start(d125[0:HP, :], dst.rearrange("(p c) -> p c", p=HP)).then_inc(ld_d125, 16)
            sp.wait_ge(natz, 2)
            whole = (BC - 1) * P
            for nat, e in ((natd, dst), (nats, src)):
                sp.dma_start(nat[:, 0:whole].rearrange("p (c l) -> p c l", l=P),
                             e[0:whole * P].rearrange("(c p l) -> p c l", p=P, l=P)).then_inc(ld_nat, 16)
                sp.dma_start(nat[0:FULLB - whole, whole:whole + P],
                             e[whole * P:FULLB * P].rearrange("(p l) -> p l", l=P)).then_inc(ld_nat, 16)
                sp.dma_start(nat[FULLB - whole:NB - whole, whole:whole + E - FULLB * P],
                             e[FULLB * P:E].rearrange("(p l) -> p l", p=1)).then_inc(ld_nat, 16)
            sp.dma_start(b0_sb[:, :], b0.rearrange("(a d) -> a d", a=1).broadcast_to((P, D))).then_inc(ld_small, 16)
            sp.dma_start(Br[:, :], b_l.rearrange("(a d) -> a d", a=1).broadcast_to((P, D))).then_inc(ld_small, 16)
            with nc.allow_non_contiguous_dma("512 numbers, once"):
                sp.dma_start(gcol[:, :], gamma.rearrange("(c p) -> p c", p=P)).then_inc(ld_small, 16)
                sp.dma_start(bcol[:, :], beta.rearrange("(c p) -> p c", p=P)).then_inc(ld_small, 16)
            for g in range(XG):
                t0 = g * X_GROUP
                n = X_GROUP if g < XG - 1 else X_GROUP - 1
                sp.dma_start(nodes[:, t0 * D:(t0 + n) * D].rearrange("p (t d) -> p t d", d=D),
                             x[t0 * P:(t0 + n) * P, :].rearrange("(t p) d -> p t d", p=P)).then_inc(ld_x[g], 16)
                if g == XG - 1:
                    sp.wait_ge(consts, 1)
                    sp.dma_start(nodes[0:LAST, (NT - 1) * D:NT * D], x[(NT - 1) * P:N, :]).then_inc(ld_x[g], 16)
            for n, w in enumerate((w_l, w_r)):
                sp.dma_start(wnat[:, n * KC * D:(n + 1) * KC * D].rearrange("p (c n) -> p c n", n=D),
                             w.rearrange("(c p) n -> p c n", p=P)).then_inc(wl_ld, 16)
            sp.wait_ge(nat_tr, 4)
            sp.dma_start(w0_sb[:, :].rearrange("p (c n) -> p c n", n=D),
                         W0.rearrange("(c p) n -> p c n", p=P)).then_inc(ld_w, 16)
            for t0, t1 in zip(T1_CUTS, T1_CUTS[1:]):
                sp.wait_ge(split0, t1)
                sp.dma_start(table[0][t0 * P:t1 * P, :].rearrange("(t p) c -> p t c", p=P),
                             nodes16[:, t0 * 2 * D:t1 * 2 * D].rearrange("p (t c) -> p t c", c=2 * D)
                             ).then_inc(t1_stored, 16)
            for l in range(2):
                with sp.Fori(0, GROUPS) as g:
                    for j in range(RING):
                        sp.wait_ge(got[l][j], g * 16 + 16)
                        if j % QUAD == QUAD - 1:
                            sp.sem_inc(arrived[l], 1)

        @block.gpsimd
        def _(pool):
            pool.iota(iotaf[:, :], [[1, P]], base=0, channel_multiplier=0,
                      allow_small_or_imprecise_dtypes=True).then_inc(iota_ok, 1)
            pool.memset(natd, -1).then_inc(natz, 1)
            pool.memset(nats, 0).then_inc(natz, 1)
            pool.memset(nodes[:, (NT - 1) * D:NT * D], 0.0).then_inc(consts, 1)
            for t, v in ((ident, 0.0), (ident16, 0.0), (zero16, 0.0), (last_lane, 1.0), (eps, EPS), (one_c, 1.0)):
                pool.memset(t[:, :], v).then_inc(consts, 1)
            pool.iota(tile0[:, :], [[P, NT]], base=0, channel_multiplier=0,
                      allow_small_or_imprecise_dtypes=True).then_inc(consts, 1)
            pool.iota(thr[:, :], [[0, 1]], base=P, channel_multiplier=P,
                      allow_small_or_imprecise_dtypes=True).then_inc(consts, 1)
            pool.wait_ge(consts, 9)
            for m in (ident, ident16):
                pool.affine_select(out=m[:, :], in_=m[:, :], compare_op=ALU.not_equal, fill=1.0,
                                   base=0, pattern=[[-1, P]], channel_multiplier=1).then_inc(consts, 1)
            pool.affine_select(out=last_lane[:, :], in_=last_lane[:, :], compare_op=ALU.is_ge, fill=0.0,
                               base=-(P - 1), pattern=[[0, P]], channel_multiplier=1).then_inc(consts, 1)
            with pool.Fori(0, NT // 8) as eight:
                for h in range(2):
                    T = eight * 8 + h * 4 + 3
                    pool.wait_ge(t_made, T + 1)
                    pool.tensor_copy(nodes16[:, ds(T * 2 * D, D)], t32_of(h * 4 + 3)).then_inc(hip_made, 1)

            for l in range(2):
                if l == 0:
                    pool.wait_ge(t1_stored, 16 * (len(T1_CUTS) - 1))
                    pool.wait_ge(meta, 2)
                else:
                    pool.wait_ge(t2_stored, 16 * NT)
                    pool.wait_ge(arrived[0], NQ)
                    pool.wait_ge(s_free[0], STEPS + SQ)
                pool.sem_inc(freed[l], RQ)

                def gather_round(g, q):
                    for j in range(RING):
                        if j % QUAD == 0:
                            pool.wait_ge(freed[l], g * RQ + (j // QUAD + 1))
                            pool.sem_inc(passed, 1)
                        if j == 0:
                            pool.tensor_copy(idx[:, q * RING:(q + 1) * RING], srcT[:, ds(g * RING, RING)]).then_inc(idx_set[l], 1)
                            pool.wait_ge(idx_set[l], g + 1)
                            pool.sem_inc(passed, 1)
                        c = q * RING + j
                        pool.indirect_dma_start(
                            out=ring[:, j * 2 * D:(j + 1) * 2 * D], out_offset=None, in_=table[l],
                            in_offset=bass.IndirectOffsetOnAxis(ap=idx[:, c:c + 1], axis=0)).then_inc(got[l][j], 16)

                assert GROUPS % 2 == 1
                with pool.Fori(0, GROUPS - 1, 2) as g:
                    gather_round(g, 0)
                    gather_round(g + 1, 1)
                gather_round(GROUPS - 1, 0)

        def live(T, back, count=NT):
            return not isinstance(T, int) or 0 <= T - back < count

        def own_terms(l, T, back):
            n = l * BETWEEN
            for turn, count in TURNS[l]:
                if isinstance(T, int) and T - back == turn:
                    return range(n, n + count)
                n += count
            return range(0)

        def is_early(T, loop):
            return T >= EARLY if isinstance(T, int) else loop == 1

        def tiles(eng, body, first, drain, cut=None):
            for T in range(first):
                body(T, T % 2)
            assert NT % 2 == 1 and first % 2 == 0
            if cut is None:
                with eng.Fori(first, NT - 1, 2) as T:
                    body(T, 0)
                    body(T + 1, 1)
            else:
                assert cut % 2 == 0
                with eng.Fori(first, cut, 2) as T:
                    body(T, 0, 0)
                    body(T + 1, 1, 0)
                for T in range(cut, cut + 4):
                    body(T, T % 2)
                with eng.Fori(cut + 4, NT - 1, 2) as T:
                    body(T, 0, 1)
                    body(T + 1, 1, 1)
            for T in range(NT - 1, NT + drain):
                body(T, T % 2)

        @block.scalar
        def _(act):
            act.wait_ge(iota_ok, 1)
            nc.scalar.activation(iotax[:, NT * HIST_COLS:].rearrange("p (v c) -> p v c", c=HIST_COLS),
                                 iotaf[:, :].rearrange("p (v c) -> p v c", c=1).broadcast_to((P, P, HIST_COLS)),
                                 ACT.Copy).then_inc(digits, 1)
            act.wait_ge(ld_nat, 96)
            nc.scalar.activation(natf[:, 0:BC * P], natd, ACT.Copy).then_inc(nat_cast, 1)
            nc.scalar.activation(natf[:, BC * P:2 * BC * P], nats, ACT.Copy).then_inc(nat_cast, 1)

            def copy_edges():
                act.wait_ge(nat_tr, 4)
                for k, bk in enumerate(EDGE_BANKS):
                    b = k % 2 * 512
                    n = min(512, NQ * QUAD - b)
                    nc.scalar.activation((dstT, srcT)[k // 2][:, b:b + n], bk[:, 0:n], ACT.Copy).then_inc(nat_cp, 1)

            act.wait_ge(consts, 12)
            passes = [0]

            def summed(T, func, into, **more):
                unused = passes[0] % 2 * 512
                if passes[0] >= 2:
                    act.wait_ge(var_ok, passes[0] - 1)
                passes[0] += 1
                nc.scalar.activation(aggp[:, unused:unused + D], nodes[:, T * D:(T + 1) * D], func,
                                     accum_out=into[:, T:T + 1], **more).then_inc(var_ok, 1)

            for g in range(XG):
                if g == 1:
                    copy_edges()
                act.wait_ge(ld_x[g], 32 if g == XG - 1 else 16)
                t0 = g * X_GROUP
                for T in range(t0, t0 + X_GROUP):
                    summed(T, ACT.Copy, sum0)
                act.wait_ge(var_ok, passes[0])
                nc.scalar.activation(nmean0[:, t0:t0 + X_GROUP], sum0[:, t0:t0 + X_GROUP], ACT.Copy,
                                     scale=-1.0 / D).then_inc(mean_ok, 1)
                act.wait_ge(mean_ok, g + 1)
                for T in range(t0, t0 + X_GROUP):
                    summed(T, ACT.Square, ssq0, bias=nmean0[:, T:T + 1])
            act.wait_ge(var_ok, 2 * NT)
            nc.scalar.activation(sdx, ssq0, ACT.Sqrt, bias=eps[:, :], scale=1.0 / D).then_inc(sdx_ok, 1)
            act.wait_ge(deg_ok, 1)
            nc.scalar.activation(sdeg, deg, ACT.Sqrt).then_inc(sdeg_ok, 1)
            act.wait_ge(scale_ok, 1)

            def scaled(T, q):
                if live(T, 8):
                    act.wait_ge(split0, T - 7)
                nc.scalar.activation(t32_of(q), nodes[:, ds(T * D, D)], ACT.Relu,
                                     bias=bias0[:, ds(T, 1)], scale=scale0[:, ds(T, 1)]).then_inc(t_made, 1)

            assert NT % 8 == 1
            for T in range(8):
                scaled(T, T)
            with act.Fori(1, NT // 8) as eight:
                for q in range(8):
                    scaled(eight * 8 + q, q)
            scaled(NT - 1, 0)

            def distances(l, T, qd):
                act.wait_ge(s_ready[l], qd + T + 1)
                o = ((qd + T) & 1) * (QUAD * P)
                for j in range(QUAD):
                    ins = nc.scalar.activation(absd[:, ds(o + j * P, P)], iota_t[:, :], ACT.Abs,
                                               bias=dstT[:, ds(qd * QUAD + j, 1)], scale=-1.0)
                ins.then_inc(s_abs[l], 1)

            def matrices(l, T, qd):
                act.wait_ge(s_abs[l], qd + T + 1)
                act.wait_ge(s_free[l], qd + T + 1)
                nc.scalar.activation(sel[:, ds(((qd + T) & (SQ - 1)) * (QUAD * P), QUAD * P)],
                                     absd[:, ds(((qd + T) & 1) * (QUAD * P), QUAD * P)], ACT.Relu,
                                     bias=one_c[:, :], scale=-1.0).then_inc(s_ready[l], 1)

            def start_selection(l, T):
                nc.scalar.activation(iota_t[:, :], iotaf[:, :], ACT.Identity, bias=tile0[:, ds(T, 1)]).then_inc(s_iota[l], 1)
                lo = act.value_load(tile_quad[0:1, ds(T, 1)], min_val=0, max_val=NQ - 1)
                hi = act.value_load(tile_quad[0:1, ds(T + 1, 1)], min_val=0, max_val=NQ - 1)
                act.wait_ge(s_iota[l], T + 1)
                distances(l, T, lo)
                return lo, hi

            def finish_selection(l, T, lo, hi):
                with act.If(lo < hi):
                    with act.Fori(lo, hi) as qd:
                        distances(l, T, qd + 1)
                        matrices(l, T, qd)
                matrices(l, T, hi)

            def load_x(T):
                act.wait_ge(agg_done[0], T + 1)
                if live(T, 1):
                    act.wait_ge(tin_ld[0], T * 16)
                rows = LAST if isinstance(T, int) and T == NT - 1 else P
                act.dma_start(nodes[0:rows, ds(T * D, D)], x[ds(T * P, rows), :]).then_inc(tin_ld[0], 16)

            def store_table(T, q):
                act.wait_ge(split_ok, T + 1)
                if live(T, 1):
                    act.wait_ge(t2_stored, T * 16)
                act.dma_start(table[1][ds(T * P, P), :], stage[:, q * 2 * D:(q + 1) * 2 * D]).then_inc(t2_stored, 16)

            def copy_zT(T, q):
                act.wait_ge(z_tr, T + 1)
                if live(T, 1):
                    act.wait_ge(zT_stored, T * 16)
                nc.scalar.activation(zT[:, q * D:(q + 1) * D], ztp[:, :], ACT.Copy).then_inc(zT_ok, 1)

            def store_zT(T, q):
                act.wait_ge(zT_ok, T + 1)
                act.dma_start(xT_dram[ds(T * P, P), :], zT[:, q * D:(q + 1) * D]).then_inc(zT_stored, 16)

            def load_own(k):
                act.wait_ge(zT_stored, (EARLY + k + 1) * 16)
                if k >= 1:
                    act.wait_ge(own_ld, k * 16)
                if k >= 2:
                    act.wait_ge(own_mm, k - 1)
                act.dma_start(own_place(k)[0], xT_dram[(EARLY + k) * P:(EARLY + k + 1) * P, :]).then_inc(own_ld, 16)

            def store_own(k):
                act.wait_ge(own_mm, k + 1)
                if k >= 1:
                    act.wait_ge(own_stored, k * 16)
                t = own_out[:, k % 2 * D:(k % 2 + 1) * D]
                nc.scalar.activation(t, own_place(k)[1][:, :], ACT.Copy).then_inc(own_cp, 1)
                act.wait_ge(own_cp, k + 1)
                act.dma_start(xT_dram[(EARLY + k) * P:(EARLY + k + 1) * P, :], t).then_inc(own_stored, 16)

            def first_phase(T, q):
                if live(T, 0):
                    lo, hi = start_selection(0, T)
                if live(T, 7):
                    copy_zT(T - 7, 1 - q)
                if live(T, 2):
                    load_x(T - 2)
                if live(T, 6):
                    store_table(T - 6, q)
                if live(T, 7):
                    store_zT(T - 7, 1 - q)
                if isinstance(T, int) and T == TURNS[0][0][0] - 1:
                    load_own(0)
                    load_own(1)
                for k in own_terms(0, T, 2):
                    store_own(k)
                    load_own(k + 2)
                if live(T, 0):
                    finish_selection(0, T, lo, hi)

            act.wait_ge(be_row, 2)
            act.wait_ge(split0, NT)
            act.sem_inc(s_free[0], SQ)
            act.sem_inc(s_ready[0], 2)
            tiles(act, first_phase, 8, 7)
            act.wait_ge(zT_stored, 16 * NT)

            def load_own_side(T, q, early):
                if live(T, 2):
                    act.wait_ge(mm_done[1], T - 1)
                    if early:
                        act.wait_ge(tin_used[1], T - 1)
                        if isinstance(T, int) and T == EARLY:
                            act.wait_ge(own_stored, 16 * OWN)
                if live(T, 1):
                    act.wait_ge(tin_ld[1], T * 16)
                act.dma_start(xin[:, q * D:(q + 1) * D], xT_dram[ds(T * P, P), :]).then_inc(tin_ld[1], 16)

            def store_out(T, q):
                act.wait_ge(res_ok[1], T + 1)
                if live(T, 1):
                    act.wait_ge(out_stored, T * 16)
                rows = LAST if isinstance(T, int) and T == NT - 1 else P
                act.dma_start(out[ds(T * P, rows), :], res[0:rows, q * D:(q + 1) * D]).then_inc(out_stored, 16)

            def second_phase(T, q, loop=None):
                if live(T, 0):
                    lo, hi = start_selection(1, T)
                for k in own_terms(1, T, 2):
                    store_own(k)
                    if k + 2 < OWN:
                        load_own(k + 2)
                if live(T, 2) and not is_early(T - 2, loop):
                    load_own_side(T - 2, q, False)
                if live(T, 3) and is_early(T - 3, loop):
                    load_own_side(T - 3, 1 - q, True)
                if live(T, 5):
                    store_out(T - 5, 1 - q)
                if live(T, 0):
                    finish_selection(1, T, lo, hi)

            act.wait_ge(s_free[0], STEPS + SQ)
            act.sem_inc(s_free[1], SQ)
            act.sem_inc(s_ready[1], 2)
            tiles(act, second_phase, 8, 5, EARLY)
            act.wait_ge(out_stored, 16 * NT)

        @block.tensor
        def _(pe):
            pe.wait_ge(consts, 12)
            pe.wait_ge(nat_cast, 2)
            for k, bk in enumerate(EDGE_BANKS):
                for n, c in enumerate(range(k % 2 * 4, min(k % 2 * 4 + 4, BC))):
                    o = (k // 2 * BC + c) * P
                    mm = pe.transpose(bk[:, n * P:(n + 1) * P], natf[:, o:o + P], ident[:, :])
                mm.then_inc(nat_tr, 1)
            for k in range(CHUNKS):
                pe.wait_ge(oh_made, k + 1)
                o = (k % 2) * OH
                v = onehot[0:HP, o:o + OH].rearrange("p (v c) -> p v c", c=HIST_COLS)
                for c in range(HIST_COLS):
                    mm = pe.matmul(misc[0:NT, 0:P], v[:, 0:NT, c], v[:, NT:DIG, c],
                                   start=(k == 0 and c == 0), stop=(k == CHUNKS - 1 and c == HIST_COLS - 1))
                mm.then_inc(oh_used, 1)
            pe.wait_ge(nat_cp, 4)
            for k, bk in enumerate((outp, ztp)):
                pe.matmul(bk[:, 0:ENDS[k + 1] - ENDS[k]], last_lane[:, :], dstT[:, ENDS[k]:ENDS[k + 1]],
                          start=True, stop=True).then_inc(bcast, 1)
            pe.wait_ge(hist, 1)
            pe.transpose(misc2[:, 0:NT], hcnt, ident[0:NT, 0:NT]).then_inc(cnt_ok, 1)
            pe.wait_ge(be_ok, 2)
            pe.matmul(misc[0:1, 0:NT], be_c[0:NT, 0:1], ident[0:NT, 0:NT], start=True, stop=False,
                      skip_group_check=True)
            pe.matmul(misc[0:1, 0:NT], be_c[0:NT, 1:2], ident[0:NT, 0:NT], start=False, stop=True,
                      skip_group_check=True).then_inc(be_row, 1)
            pe.wait_ge(ld_w, 16)
            pe.wait_ge(split0, NT)

            def turn_weights():
                pe.wait_ge(wl_ld, 32)
                for n in range(2):
                    for c in range(KC):
                        k = n * KC + c
                        if k >= 2:
                            pe.wait_ge(w_cp, k - 1)
                        for r in range(KC):
                            o = (n * KC + r) * D + c * P
                            mm = pe.transpose((ztp, outp)[k % 2][:, r * P:(r + 1) * P], wnat[:, o:o + P], ident[:, :])
                        mm.then_inc(w_tr, 1)
                pe.wait_ge(beta_made, KC)
                pe.wait_ge(w_cp, 2 * KC)
                for w, bk in ((wl_sb, misc), (wr_sb, misc2)):
                    for c in range(KC):
                        mm = pe.matmul(bk[:, :], beta_b[:, c * P:(c + 1) * P], w[:, c * D:(c + 1) * D],
                                       start=(c == 0), stop=(c == KC - 1))
                    mm.then_inc(bias_mm, 1)

            def gathered(l, T, q):
                a = aggp[:, q * 512:(q + 1) * 512]
                first = pe.value_load(tile_block[0:1, ds(T, 1)], min_val=0, max_val=NB - 1)
                last = pe.value_load(tile_block[0:1, ds(T + 1, 1)], min_val=0, max_val=NB - 1)
                lo, hi = first >> QUAD_BITS, last >> QUAD_BITS

                def slots(qd):
                    return ((qd + T) & (SQ - 1)) * (QUAD * P), (qd & (RQ - 1)) * (QUAD * 2 * D)

                def add(at, j, start=False):
                    s, r = sel[:, ds(at[0] + j * P, P)], at[1] + j * 2 * D
                    high = pe.matmul(a, s, ring[:, ds(r, D)], start=start, stop=False, skip_group_check=True)
                    low = pe.matmul(a, s, ring[:, ds(r + D, D)], start=False, stop=False, skip_group_check=True)
                    return high, low

                def new_quad(qd):
                    pe.wait_ge(arrived[l], qd + 1)
                    pe.wait_ge(s_ready[l], qd + T + 3)
                    at = slots(qd)
                    high, low = add(at, 0)
                    high.then_inc(freed[l], 1)
                    low.then_inc(s_free[l], 1)
                    return at

                if live(T, 2):
                    pe.wait_ge(agg_out[l], T - 1)
                pe.wait_ge(arrived[l], lo + 1)
                pe.wait_ge(s_ready[l], lo + T + 3)
                at = slots(lo)
                add(at, QUAD - 1, start=True)
                with pe.If(lo < hi):
                    before = first & (QUAD - 1)
                    with pe.If(before < 3):
                        add(at, 2)
                        with pe.If(before < 2):
                            add(at, 1)
                            with pe.If(before < 1):
                                add(at, 0)
                    with pe.If(lo + 1 < hi):
                        with pe.Fori(lo + 1, hi) as qd:
                            inner = new_quad(qd)
                            for j in range(1, QUAD):
                                add(inner, j)
                    more = last & (QUAD - 1)
                    at_hi = new_quad(hi)
                    with pe.If(0 < more):
                        add(at_hi, 1)
                        with pe.If(1 < more):
                            add(at_hi, 2)
                            with pe.If(2 < more):
                                add(at_hi, 3)
                with pe.Else():
                    for j in range(QUAD - 1):
                        add(at, j)
                if l == 0:
                    pe.matmul(a, ident16[:, :], nodes16[:, ds(T * 2 * D, D)], start=False, stop=False,
                              skip_group_check=True).then_inc(s_free[l], 1)
                    mm = pe.matmul(a, ident16[:, :], nodes16[:, ds(T * 2 * D + D, D)], start=False, stop=True,
                                   skip_group_check=True)
                else:
                    pe.matmul(a[:, 0:2], ident16[:, :], zero16[:, :], start=False, stop=False,
                              skip_group_check=True).then_inc(s_free[l], 1)
                    mm = pe.matmul(a, ident16[:, :], zero16[:, 0:1].broadcast_to((P, D)), start=False, stop=True, skip_group_check=True)
                mm.then_inc(agg_done[l], 1)

            def turn_agg(l, T, q):
                pe.wait_ge(agg_out[l], T + 1)
                if live(T, 1):
                    pe.wait_ge(aggT_ok[l], T)
                for c in range(KC):
                    mm = pe.transpose(trp[:, c * P:(c + 1) * P], agg[:, q * D + c * P:q * D + (c + 1) * P], ident[:, :])
                mm.then_inc(agg_tr[l], 1)

            def project(l, T, q, w, more=None):
                pe.wait_ge(aggT_ok[l], T + 1)
                if isinstance(T, int) and T == 0 and l == 0:
                    pe.wait_ge(w_done, 2 * KC)
                if live(T, 2):
                    pe.wait_ge(mm_read[l], T - 1)
                out2 = outs[q]
                for c in range(KC):
                    mm = pe.matmul(out2[:, :], aggT[:, c * P:(c + 1) * P], w[:, c * D:(c + 1) * D],
                                   start=(c == 0), stop=(c == KC - 1 and more is None))
                if more is not None:
                    pe.wait_ge(tin_ld[l], T * 16 + 16)
                    for c in range(KC):
                        mm = pe.matmul(out2[:, :], xin[:, q * D + c * P:q * D + (c + 1) * P], more[:, c * D:(c + 1) * D],
                                       start=False, stop=(c == KC - 1))
                mm.then_inc(mm_done[l], 1)

            def own_term(k):
                if k == 0:
                    pe.wait_ge(w_done, 2 * KC)
                    pe.wait_ge(aggT_ok[0], NT)
                pe.wait_ge(own_ld, k * 16 + 16)
                if k >= 2:
                    pe.wait_ge(own_cp, k - 1)
                z, bk = own_place(k)
                for c in range(KC):
                    mm = pe.matmul(bk[:, :], z[:, c * P:(c + 1) * P], wr_sb[:, c * D:(c + 1) * D],
                                   start=(c == 0), stop=(c == KC - 1))
                mm.then_inc(own_mm, 1)

            def turn_z(T):
                pe.wait_ge(res_ok[0], T + 1)
                if live(T, 1):
                    pe.wait_ge(zT_ok, T)
                for c in range(KC):
                    mm = pe.transpose(ztp[:, c * P:(c + 1) * P], zs[:, c * P:(c + 1) * P], ident[:, :])
                mm.then_inc(z_tr, 1)

            def first_phase(T, q):
                if live(T, 0):
                    gathered(0, T, q)
                if live(T, 5):
                    turn_z(T - 5)
                if live(T, 2):
                    project(0, T - 2, q, w0_sb)
                if live(T, 1):
                    turn_agg(0, T - 1, 1 - q)
                for k in own_terms(0, T, 0):
                    own_term(k)

            def second_phase(T, q, loop=None):
                if live(T, 0):
                    gathered(1, T, q)
                if live(T, 2):
                    project(1, T - 2, q, wl_sb, None if is_early(T - 2, loop) else wr_sb)
                if live(T, 1):
                    if isinstance(T, int) and T == 1:
                        pe.wait_ge(own_cp, BETWEEN)
                    turn_agg(1, T - 1, 1 - q)
                for k in own_terms(1, T, 0):
                    own_term(k)

            turn_weights()
            tiles(pe, first_phase, 6, 5)
            pe.wait_ge(agg_out[0], NT)
            pe.wait_ge(w_done, 2 * KC)
            tiles(pe, second_phase, 6, 2, EARLY)

        @block.vector
        def _(dve):
            v = nc.vector
            link_n = [0]

            def link(ins):
                link_n[0] += 1
                ins.then_inc(dchain, 1)
                dve.wait_ge(dchain, link_n[0])

            v.memset(tile_block[0:1, 0:1], 0).then_inc(meta, 1)
            v.memset(be_c[:, :], 0.0).then_inc(meta, 1)
            dve.wait_ge(iota_ok, 1)
            v.tensor_copy(iotax[:, 0:NT * HIST_COLS].rearrange("p (v c) -> p v c", c=HIST_COLS),
                          iotaf[:, 0:NT].rearrange("p (v c) -> p v c", c=1).broadcast_to((P, NT, HIST_COLS))).then_inc(digits, 1)
            dve.wait_ge(ld_d125, 16)
            v.tensor_scalar(dig_i[0:HP, 0:HC], d125[0:HP, :], 7, None, ALU.arith_shift_right).then_inc(digits, 1)
            v.tensor_scalar(dig_i[0:HP, HC:2 * HC], d125[0:HP, :], P - 1, None, ALU.bitwise_and).then_inc(digits, 1)
            dve.wait_ge(digits, 4)
            v.tensor_copy(dig[0:HP, :], dig_i[0:HP, :]).then_inc(digits, 1)
            dve.wait_ge(digits, 5)
            for k in range(CHUNKS):
                if k >= 2:
                    dve.wait_ge(oh_used, k - 1)
                o = (k % 2) * OH
                for a, n, d0 in ((0, NT, 0), (NT, P, HC)):
                    ins = v.tensor_tensor(
                        onehot[0:HP, o + a * HIST_COLS:o + (a + n) * HIST_COLS].rearrange("p (v c) -> p v c", c=HIST_COLS),
                        dig[0:HP, d0 + k * HIST_COLS:d0 + (k + 1) * HIST_COLS].rearrange("p (a c) -> p a c", a=1).broadcast_to((HP, n, HIST_COLS)),
                        iotax[0:HP, a * HIST_COLS:(a + n) * HIST_COLS].rearrange("p (v c) -> p v c", c=HIST_COLS),
                        ALU.is_equal)
                ins.then_inc(oh_made, 1)
            dve.wait_ge(sdx_ok, 1)
            link(v.reciprocal(rstd0, sdx))
            link(v.tensor_scalar(rstd0, rstd0, UP, None, ALU.mult))
            dve.wait_ge(oh_used, CHUNKS)
            v.tensor_copy(hcnt, misc[0:NT, 0:P]).then_inc(hist, 1)
            dve.wait_ge(bcast, 2)
            dve.wait_ge(hist, 1)
            for k, bk in enumerate((outp, ztp)):
                n = ENDS[k + 1] - ENDS[k]
                v.tensor_scalar(agg[:, k * 512:k * 512 + n], bk[:, 0:n], thr[:, :], 0.0, ALU.is_lt, ALU.add,
                                accum_out=be_c[:, k:k + 1]).then_inc(be_ok, 1)
            dve.wait_ge(cnt_ok, 1)
            link(v.tensor_copy(cnt[:, :], misc2[:, 0:NT]))
            v.tensor_scalar(deg, cnt[:, :], 1.0, None, ALU.add).then_inc(deg_ok, 1)
            dve.wait_ge(be_row, 1)
            dve.wait_ge(meta, 2)
            link(v.tensor_copy(tile_block[0:1, 1:NT + 1], misc[0:1, 0:NT]))
            v.tensor_scalar(tile_quad[0:1, :], tile_block[0:1, :], QUAD_BITS, None,
                            ALU.arith_shift_right).then_inc(be_row, 1)
            dve.wait_ge(sdeg_ok, 1)
            link(v.reciprocal(dinv, sdeg))
            link(v.tensor_tensor(scale0, rstd0, dinv, ALU.mult))
            v.tensor_tensor(bias0, nmean0, scale0, ALU.mult).then_inc(scale_ok, 1)
            link(v.tensor_scalar(dinv_up, dinv, 1.0 / UP, None, ALU.mult))
            link(v.tensor_scalar(has, cnt[:, :], 1.0, None, ALU.min))
            link(v.tensor_scalar(cinv_up, cnt[:, :], 1.0, None, ALU.max))
            link(v.reciprocal(cinv_up, cinv_up))
            link(v.tensor_scalar(cinv_up, cinv_up, 1.0 / UP, None, ALU.mult))

            def high(T, q, highs):
                dve.wait_ge(t_made, T + 1)
                v.tensor_copy(nodes16[:, ds(T * 2 * D, D)], t32_of(q)).then_inc(hi_made, 1)

            def low(T, q, highs):
                if q % 4 < 3:
                    dve.wait_ge(hi_made, highs + q % 4 + 1)
                else:
                    dve.wait_ge(hip_made, highs)
                v.tensor_tensor(nodes16[:, ds(T * 2 * D + D, D)], t32_of(q),
                                nodes16[:, ds(T * 2 * D, D)], ALU.subtract).then_inc(split0, 1)

            with dve.Fori(0, NT // 8) as eight:
                for h in range(2):
                    T = eight * 8 + h * 4
                    q = h * 4
                    before = eight * 6 + h * 3
                    high(T, q, before)
                    high(T + 1, q + 1, before)
                    low(T, q, before)
                    high(T + 2, q + 2, before)
                    low(T + 1, q + 1, before)
                    low(T + 2, q + 2, before)
                    low(T + 3, q + 3, eight * 2 + h + 1)
            high(NT - 1, 0, NT // 4 * 3)
            low(NT - 1, 0, NT // 4 * 3)

            def copy_weights():
                for n, w in enumerate((wl_sb, wr_sb)):
                    for c in range(KC):
                        k = n * KC + c
                        dve.wait_ge(w_tr, k + 1)
                        v.tensor_copy(w[:, c * D:(c + 1) * D], (ztp, outp)[k % 2][:, :]).then_inc(w_cp, 1)
                dve.wait_ge(ld_small, 64)
                for c in range(KC):
                    v.tensor_copy(beta_b[:, c * P:(c + 1) * P], bcol[:, c:c + 1].broadcast_to((P, P))).then_inc(beta_made, 1)
                dve.wait_ge(bias_mm, 2)
                link(v.tensor_copy(Bl[:, :], misc[:, :]))
                link(v.tensor_tensor(Br[:, :], misc2[:, :], Br[:, :], ALU.add))
                for w, up in ((wl_sb, 1.0), (wr_sb, 1.0 / UP)):
                    for c in range(KC):
                        v.tensor_scalar(w[:, c * D:(c + 1) * D], w[:, c * D:(c + 1) * D], gcol[:, c:c + 1], up,
                                        ALU.mult, ALU.mult).then_inc(w_done, 1)

            def evacuate(l, T, q, by):
                dve.wait_ge(agg_done[l], T + 1)
                if live(T, 2):
                    dve.wait_ge(agg_tr[l], T - 1)
                v.tensor_scalar(agg[:, q * D:(q + 1) * D], aggp[:, q * 512:(q + 1) * 512], by[:, ds(T, 1)], None,
                                ALU.mult).then_inc(agg_out[l], 1)

            def copy_aggT(l, T):
                dve.wait_ge(agg_tr[l], T + 1)
                if live(T, 1):
                    dve.wait_ge(mm_done[l], T)
                v.tensor_copy(aggT, trp[:, :]).then_inc(aggT_ok[l], 1)

            y, v2, t2, u2 = (rs[:, 2 * n:2 * n + 2] for n in range(4))

            A_STEPS, B_STEPS = 6, 16

            def norms(a, b, qa):
                na, nb = [0], [0]

                def a_done(ins):
                    na[0] += 1
                    ins.then_inc(va, 1)

                def b_done(ins):
                    nb[0] += 1
                    ins.then_inc(vb, 1)

                def a_before():
                    dve.wait_ge(va, a * A_STEPS + na[0])

                def b_before():
                    dve.wait_ge(vb, b * B_STEPS + nb[0])

                ma, mb = 4 * qa, 4 * (1 - qa)
                ga, gb = g1[:, qa * D:(qa + 1) * D], g1[:, (1 - qa) * D:(2 - qa) * D]
                so = (1 - qa) * 2 * D
                xa = None if a is None else nodes[:, ds(a * D, D)]
                xb = None if b is None else nodes[:, ds(b * D, D)]
                if a is not None:
                    dve.wait_ge(mm_done[0], a + 1)
                    v.tensor_tensor(act_sum, outs[qa][:, :], b0_sb[:, :], ALU.add).then_inc(mm_read[0], 1)
                if b is not None:
                    b_done(v.tensor_scalar(v2[:, 0:1], mv[:, mb + 1:mb + 2], EPS, None, ALU.add))
                if a is not None:
                    dve.wait_ge(mm_read[0], a + 1)
                    dve.wait_ge(tin_ld[0], a * 16 + 16)
                    a_done(v.scalar_tensor_tensor(xa, act_sum, 0.0, xa, ALU.max, ALU.add))
                if b is not None:
                    b_before()
                    b_done(v.scalar_tensor_tensor(v2[:, 1:2], v2[:, 0:1], EPS, mv[:, mb + 3:mb + 4], ALU.mult, ALU.add))
                if a is not None:
                    a_before()
                    dve.sem_inc(passed_v, 1)
                    a_done(v.bn_stats(st[:, 0:6], xa))
                if b is not None:
                    b_before()
                    b_done(v.tensor_scalar(t2.bitcast(I32), v2.bitcast(I32), 1, None, ALU.arith_shift_right))
                if a is not None:
                    a_before()
                    dve.sem_inc(passed_v, 1)
                    a_done(v.bn_aggr(mv[:, ma:ma + 2], st[:, 0:6]))
                if b is not None:
                    b_before()
                    b_done(v.tensor_scalar(y.bitcast(I32), t2.bitcast(I32), -1.0, float(0x5F3759DF), ALU.mult, ALU.add))
                if a is not None:
                    a_before()
                    a_done(v.tensor_scalar(ga, xa, mv[:, ma:ma + 1], mv[:, ma:ma + 1], ALU.max, ALU.subtract))
                for n in range(NEWTON):
                    if b is not None:
                        b_before()
                        b_done(v.scalar_tensor_tensor(t2, y, -0.5, v2, ALU.mult, ALU.mult))
                    if n == 0 and a is not None:
                        a_before()
                        a_done(v.bn_stats(st[:, 6:12], ga))
                    if b is not None:
                        b_before()
                        b_done(v.tensor_tensor(u2, t2, y, ALU.mult))
                    if n == 0 and a is not None:
                        a_before()
                        dve.sem_inc(passed_v, 1)
                        a_done(v.bn_aggr(mv[:, ma + 2:ma + 4], st[:, 6:12]))
                    if b is not None:
                        b_before()
                        b_done(v.scalar_tensor_tensor(y, u2, 1.5, y, ALU.add, ALU.mult))
                if b is not None:
                    b_before()
                    b_done(v.tensor_scalar(u2[:, 1:2], y[:, 1:2], UP, None, ALU.mult))
                    b_before()
                    if live(b, 1):
                        dve.wait_ge(z_tr, b)
                    b_done(v.tensor_scalar(zs, gb, mv[:, mb + 2:mb + 3], u2[:, 1:2], ALU.subtract, ALU.mult))
                    v.scalar_tensor_tensor(xb, gb, y[:, 0:1], xb, ALU.mult, ALU.add).then_inc(res_ok[0], 1)
                    if live(b, 2):
                        dve.wait_ge(t2_stored, (b - 1) * 16)
                    b_before()
                    b_done(v.tensor_copy(stage[:, so:so + D], zs))
                    b_before()
                    v.tensor_tensor(stage[:, so + D:so + 2 * D], zs, stage[:, so:so + D],
                                    ALU.subtract).then_inc(split_ok, 1)
                assert na[0] in (0, A_STEPS) and nb[0] in (0, B_STEPS)

            def first_phase(T, q):
                if live(T, 0):
                    evacuate(0, T, q, dinv_up)
                if live(T, 3) or live(T, 4):
                    norms(T - 3 if live(T, 3) else None, T - 4 if live(T, 4) else None, 1 - q)
                if live(T, 1):
                    copy_aggT(0, T - 1)

            def result(T, q, early):
                dve.wait_ge(mm_done[1], T + 1)
                v.scalar_tensor_tensor(act_sum, Bl[:, :], has[:, ds(T, 1)], outs[q][:, :], ALU.mult, ALU.add).then_inc(mm_read[1], 1)
                dve.wait_ge(mm_read[1], T + 1)
                if early:
                    dve.wait_ge(tin_ld[1], T * 16 + 16)
                    v.tensor_tensor(x1, act_sum, xin[:, q * D:(q + 1) * D], ALU.add).then_inc(own_used, 1)
                    dve.wait_ge(own_used, T - EARLY + 1)
                    v.tensor_tensor(x1, x1, Br[:, :], ALU.add).then_inc(tin_used[1], 1)
                else:
                    v.tensor_tensor(x1, act_sum, Br[:, :], ALU.add).then_inc(tin_used[1], 1)
                dve.wait_ge(tin_used[1], T + 1)
                if live(T, 2):
                    dve.wait_ge(out_stored, (T - 1) * 16)
                else:
                    dve.wait_ge(t2_stored, NT * 16)
                v.scalar_tensor_tensor(res[:, q * D:(q + 1) * D], x1, 0.0, nodes[:, ds(T * D, D)], ALU.max,
                                       ALU.add).then_inc(res_ok[1], 1)

            def second_phase(T, q, loop=None):
                if live(T, 0):
                    evacuate(1, T, q, cinv_up)
                if live(T, 3):
                    result(T - 3, 1 - q, is_early(T - 3, loop))
                if live(T, 1):
                    copy_aggT(1, T - 1)

            copy_weights()
            tiles(dve, first_phase, 6, 4)
            tiles(dve, second_phase, 6, 3, EARLY)


_INS = ['x', 'src', 'dst', 'L0_gnn_W', 'L0_gnn_b', 'L1_gnn_ln_gamma', 'L1_gnn_ln_beta', 'L1_gnn_w_l', 'L1_gnn_b_l', 'L1_gnn_w_r']


def kernel(**inputs):
    import numpy as _np
    import concourse.bacc as _bacc
    from concourse import mybir as _mybir
    from concourse.bass_utils import run_bass_kernel_spmd as _run

    nc = _bacc.Bacc("TRN2", target_bir_lowering=False, num_devices=1)
    arrays, args = {}, []
    for name in _INS:
        a = _np.ascontiguousarray(inputs[name])
        arrays[f"in_{name}_dram"] = a
        args.append(nc.dram_tensor(f"in_{name}_dram", a.shape, _mybir.dt.from_np(a.dtype), kind="ExternalInput").ap())
    shape = inputs['x'].shape
    out = nc.dram_tensor("out_0_dram", shape, _mybir.dt.float32, kind="ExternalOutput").ap()
    gnn_kernel(nc, *args, out)
    r = _run(nc, [arrays], core_ids=[0])
    return r.results[0]["out_0_dram"]
```
